# Optimizing a Trainium2 kernel written in Bass

```python
import numpy as np
import jax
import jax.numpy as jnp

def _softmax(x, axis=-1):
    return jax.nn.softmax(x, axis=axis)

def _gelu(x):
    return jax.nn.gelu(x, approximate=True)

def _silu(x):
    return jax.nn.silu(x)

def _sigmoid(x):
    return jax.nn.sigmoid(x)

def _layernorm(x, axis=-1, eps=1e-05):
    m = jnp.mean(x, axis=axis, keepdims=True)
    v = jnp.var(x, axis=axis, keepdims=True)
    return (x - m) / jnp.sqrt(v + eps)

def _scatter_add(tgt, idx, src, axis=0):
    return tgt.at[idx].add(src)

def _segment_sum(src, seg, n):
    return jax.ops.segment_sum(src, seg, n)
kernel_name = 'mk_conv_preact_d1_conv_nchw256_r2_0708f7'

def setup_inputs(seed: int=0):
    np.random.seed(seed)
    _w = jnp.asarray

    def _rec_inputs():
        import jax
        import jax.numpy as jnp
        _gk = jax.random.key(seed)
        x = 7.22e-05 + 1 * jax.random.normal(jax.random.fold_in(_gk, 1), (32, 128, 32, 32), jnp.float32)
        return x
    x = _rec_inputs()

    def _L0_conv_setup():
        import jax, jax.numpy as jnp
        import numpy as np
        EPS = 1e-05

        def _bn(x, gamma, beta, axes, ch_shape):
            mean = jnp.mean(x, axis=axes, keepdims=True)
            var = jnp.var(x, axis=axes, keepdims=True)
            xn = (x - mean) * jax.lax.rsqrt(var + EPS)
            return xn * gamma.reshape(ch_shape) + beta.reshape(ch_shape)
        key = jax.random.key(seed)
        ks = jax.random.split(key, 5)
        b, d, n1, n2 = (32, 128, 32, 32)
        k_dim, h, v = (16, 4, 32)
        n = n1 * n2
        m = n
        std_kv = 1.0 / np.sqrt(d)
        std_q = 1.0 / np.sqrt(d * k_dim)
        return {'x': jax.random.normal(ks[0], (b, d, n1, n2), jnp.float32), 'Wq': jax.random.normal(ks[1], (k_dim * h, d), jnp.float32) * std_q, 'Wk': jax.random.normal(ks[2], (k_dim, d), jnp.float32) * std_kv, 'Wv': jax.random.normal(ks[3], (v, d), jnp.float32) * std_kv, 'E': jax.random.normal(ks[4], (n, m, k_dim), jnp.float32), 'gamma_v': jnp.ones((m,), jnp.float32), 'beta_v': jnp.zeros((m,), jnp.float32), 'gamma_q': jnp.ones((k_dim,), jnp.float32), 'beta_q': jnp.zeros((k_dim,), jnp.float32)}
    _L0_conv_all = _L0_conv_setup()
    _L0_conv_in = {k: v for k, v in _L0_conv_all.items() if k in ('Wq', 'Wk', 'Wv', 'E', 'gamma_v', 'beta_v', 'gamma_q', 'beta_q')}
    del _L0_conv_all
    return {'x': x, 'L0_conv_Wq': _L0_conv_in['Wq'], 'L0_conv_Wk': _L0_conv_in['Wk'], 'L0_conv_Wv': _L0_conv_in['Wv'], 'L0_conv_E': _L0_conv_in['E'], 'L0_conv_gamma_v': _L0_conv_in['gamma_v'], 'L0_conv_beta_v': _L0_conv_in['beta_v'], 'L0_conv_gamma_q': _L0_conv_in['gamma_q'], 'L0_conv_beta_q': _L0_conv_in['beta_q']}

def reference(x, L0_conv_Wq, L0_conv_Wk, L0_conv_Wv, L0_conv_E, L0_conv_gamma_v, L0_conv_beta_v, L0_conv_gamma_q, L0_conv_beta_q):
    import jax
    import jax.numpy as jnp

    def _L0_conv_ref(x, Wq, Wk, Wv, E, gamma_v, beta_v, gamma_q, beta_q):
        import jax, jax.numpy as jnp
        import numpy as np
        EPS = 1e-05

        def _bn(x, gamma, beta, axes, ch_shape):
            mean = jnp.mean(x, axis=axes, keepdims=True)
            var = jnp.var(x, axis=axes, keepdims=True)
            xn = (x - mean) * jax.lax.rsqrt(var + EPS)
            return xn * gamma.reshape(ch_shape) + beta.reshape(ch_shape)
        b, d, n1, n2 = x.shape
        n = n1 * n2
        k_dim = Wk.shape[0]
        h = Wq.shape[0] // k_dim
        xf = x.reshape(b, n, d)
        keys = xf @ Wk.T
        softmax_keys = jax.nn.softmax(keys, axis=1)
        values = _bn(xf @ Wv.T, gamma_v, beta_v, axes=(0, 2), ch_shape=(1, -1, 1))
        queries = (xf @ Wq.T).reshape(b, n, k_dim, h).transpose(0, 2, 1, 3)
        queries = _bn(queries, gamma_q, beta_q, axes=(0, 2, 3), ch_shape=(1, -1, 1, 1))
        content_lambda = jnp.einsum('bmk,bmv->bkv', softmax_keys, values)
        position_lambdas = jnp.einsum('nmk,bmv->bnkv', E, values)
        content_output = jnp.einsum('bknh,bkv->bhvn', queries, content_lambda)
        position_output = jnp.einsum('bknh,bnkv->bhvn', queries, position_lambdas)
        return (content_output + position_output).reshape(b, d, n1, n2)

    def _gn(v, G=32, eps=1e-05):
        B_, C_, H_, W_ = v.shape
        g = v.reshape(B_, G, C_ // G, H_, W_)
        m = jnp.mean(g, axis=(2, 3, 4), keepdims=True)
        s = jnp.var(g, axis=(2, 3, 4), keepdims=True)
        return ((g - m) / jnp.sqrt(s + eps)).reshape(v.shape)

    def _ln_c(v, eps=1e-06):
        m = jnp.mean(v, axis=1, keepdims=True)
        s = jnp.var(v, axis=1, keepdims=True)
        return (v - m) / jnp.sqrt(s + eps)

    def _ln_t(v, eps=1e-05):
        m = jnp.mean(v, axis=-1, keepdims=True)
        s = jnp.var(v, axis=-1, keepdims=True)
        return (v - m) / jnp.sqrt(s + eps)

    def _to_tokens(v):
        B_, C_, H_, W_ = v.shape
        return v.reshape(B_, C_, H_ * W_).transpose(0, 2, 1)

    def _from_tokens(t, like):
        B_, C_, H_, W_ = like.shape
        return t.transpose(0, 2, 1).reshape(B_, C_, H_, W_)
    x = x + _L0_conv_ref(_gn(x), L0_conv_Wq, L0_conv_Wk, L0_conv_Wv, L0_conv_E, L0_conv_gamma_v, L0_conv_beta_v, L0_conv_gamma_q, L0_conv_beta_q)
    return x

_drawn_inputs = setup_inputs


def setup_inputs(seed=0):
    import zlib

    import numpy as np

    out = dict(_drawn_inputs(seed))
    spreads = {'L0_conv_gamma_v': (1.0, 0.2),
     'L0_conv_beta_v': (0.0, 0.1),
     'L0_conv_gamma_q': (1.0, 0.2),
     'L0_conv_beta_q': (0.0, 0.1)}
    factors = {'L0_conv_Wk': 8.0}
    for name, (base, spread) in spreads.items():
        noise = np.random.default_rng([zlib.crc32(name.encode()), seed]).standard_normal(out[name].shape)
        drawn = base * np.exp(spread * noise) if base else spread * noise
        out[name] = jnp.asarray(drawn.astype(out[name].dtype))
    for name, factor in factors.items():
        out[name] = (out[name] * factor).astype(out[name].dtype)
    return out
```

```python
import concourse.bass as bass
from concourse import mybir
from contextlib import ExitStack


def lambda_conv_kernel(nc: bass.Bass, x, Wq, Wk, Wv, E, gamma_v, beta_v, gamma_q, beta_q, out):
    f32 = mybir.dt.float32
    f32r = mybir.dt.float32r
    ALU = mybir.AluOpType
    ACT = mybir.ActivationFunctionType
    AX = mybir.AxisListType
    RMAX = bass.bass_isa.ReduceOp.max

    P = 128
    B, C, H, W = x.shape
    D = C
    J = H * W // D
    N = H * W
    KD = Wk.shape[0]
    NH = Wq.shape[0] // KD
    V = Wv.shape[0]
    A = P // V
    G = B // A
    BV = B * V
    BH = B * NH
    QC, KC = KD * NH, KD
    PC = QC + KC + V
    TN = P // KD
    TILES = N // TN
    BANK = 512
    BT = 16
    BLOCKS = TILES // BT
    BN = BT * TN
    PAIRS = TILES // 2
    PPB = BT // 2
    GB = 4
    GN_C = C // 32
    EPS = 1e-5

    ctx = ExitStack()

    def sb(name, shape, dt=f32, stack=ctx):
        return stack.enter_context(nc.sbuf_tensor(name, shape, dt))

    with ctx:
        ident = sb("ident", [P, P])
        group_avg = sb("group_avg", [P, P])
        same_k = sb("same_k", [P, P])
        row_mask = sb("row_mask", [P, TN])
        fold = sb("fold", [P, KD])
        ones = sb("ones", [P, 1])
        inv_p = sb("inv_p", [P, 1])
        eps_t = sb("eps_t", [P, 1])
        w_rows = sb("w_rows", [PC, D])
        w_cols = sb("w_cols", [D, PC])
        gam_v = sb("gam_v", [P, J])
        bet_v = sb("bet_v", [P, J])
        gam_q = sb("gam_q", [P, 1])
        bet_q = sb("bet_q", [P, 1])
        bn6 = sb("bn6", [P, 2 * GB, 2, 6])
        mv = sb("mv", [P, 2, GB, 2])
        gn_in = sb("gn_in", [P, 2, GB, 2])
        gn_sq = sb("gn_sq", [P, 2, GB])
        gn_out = sb("gn_out", [P, 2, GB, 2])
        gn_var = sb("gn_var", [P, 2, GB])
        gn_std = sb("gn_std", [P, 2, GB])
        gn_rstd = sb("gn_rstd", [P, 2, GB])
        gn_bias = sb("gn_bias", [P, 2, GB])
        v_stats = sb("v_stats", [P, J, A, 6])
        q_stats = sb("q_stats", [P, KD, A, 6])
        v_mv = sb("v_mv", [P, J, 2])
        v_std = sb("v_std", [P, J])
        v_scale = sb("v_scale", [P, J])
        v_tmp = sb("v_tmp", [P, J])
        v_shift = sb("v_shift", [P, J])
        q_mv = sb("q_mv", [P, KD, 2])
        q_in = sb("q_in", [P, 2, TN, KD])
        q_sq = sb("q_sq", [P, KD])
        q_out = sb("q_out", [P, 2])
        q_tmp = sb("q_tmp", [P, 4])
        q_scale = sb("q_scale", [P, 1])
        q_shift = sb("q_shift", [P, 1])
        key_max = sb("key_max", [P, B * KD])
        key_top = sb("key_top", [P, B * KD])
        exp_sum = sb("exp_sum", [P, B * KD])
        inv_sum = sb("inv_sum", [P, B // TN])
        lam_diag = sb("lam_diag", [P, BV])
        content = sb("content", [P, BV])
        qn = sb("qn", [P, 2, BH])
        e_nat = sb("e_nat", [P, 2, 2 * TN, J * KD])
        e_hi = sb("e_hi", [P, 2, J, TN, KD], f32r)
        e_lo = sb("e_lo", [P, 2, J, TN, KD], f32r)

        keys = sb("keys", [P, J, G, A, KD])
        early = ExitStack()
        x_in = sb("x_in", [P, 2 * GB, J * D], stack=early)
        x_t = sb("x_t", [D, 2, J * C], stack=early)
        early.close()
        v_hi = sb("v_hi", [P, J, BV], f32r)
        v_lo = sb("v_lo", [P, J, BV], f32r)
        early = ExitStack()
        q_nat = sb("q_nat", [P, 2, J, KD, G, NH], stack=early)
        v_nat = sb("v_nat", [P, J, G, A, V], stack=early)
        early.close()
        q_in_blk = sb("q_in_blk", [P, 2 * BT, BH])
        pos = sb("pos", [P, 2, BV])
        q_diag = sb("q_diag", [P, 2, B * NH * TN])
        res = sb("res", [P, G * NH, 2 * BN])

        ps_a = ctx.enter_context(nc.psum_tensor("ps_a", [P, 2, BV], f32))
        ps_b = ctx.enter_context(nc.psum_tensor("ps_b", [P, 2, BV], f32))
        q_dram = nc.dram_tensor("q_dram", (C, J * KD, A, G * NH), f32).ap()
        gn_ps = ps_b[:, 1, 0:2 * GB]

        def sem(name):
            return ctx.enter_context(nc.semaphore(name))

        x_loaded = [sem(f"x_loaded{i}") for i in range(2 * GB)]
        weights_loaded = sem("weights_loaded")
        params_loaded = sem("params_loaded")
        memsets = sem("memsets")
        consts = sem("consts")
        w_transposed = sem("w_transposed")
        w_ready = sem("w_ready")
        same_k_ready = sem("same_k_ready")
        gn_stats = sem("gn_stats")
        gn_summed = sem("gn_summed")
        gn_read = sem("gn_read")
        gn_var_ready = sem("gn_var_ready")
        gn_std_ready = sem("gn_std_ready")
        gn_ready = sem("gn_ready")
        x_normed = sem("x_normed")
        x_transposed = sem("x_transposed")
        xt_ready = sem("xt_ready")
        projected = sem("projected")
        proj_read = sem("proj_read")
        q_stats_done = sem("q_stats_done")
        q_stored = [sem(f"q_stored{i}") for i in range(2)]
        dve_step = sem("dve_step")
        v_var_ready = sem("v_var_ready")
        v_std_ready = sem("v_std_ready")
        v_affine = sem("v_affine")
        v_normed = sem("v_normed")
        v_hi_ready = sem("v_hi_ready")
        v_lo_ready = sem("v_lo_ready")
        key_max_ready = sem("key_max_ready")
        key_top_ready = sem("key_top_ready")
        keys_shifted = sem("keys_shifted")
        keys_exp = sem("keys_exp")
        exp_summed = sem("exp_summed")
        q_moments = sem("q_moments")
        q_averaged = sem("q_averaged")
        q_var_ready = sem("q_var_ready")
        q_std_ready = sem("q_std_ready")
        q_affine = sem("q_affine")
        lam_summed = sem("lam_summed")
        lam_masked = sem("lam_masked")
        lam_spread = sem("lam_spread")
        e_loaded = [sem(f"e_loaded{i}") for i in range(2)]
        e_hi_ready = sem("e_hi_ready")
        e_lo_ready = sem("e_lo_ready")
        pos_summed = sem("pos_summed")
        pos_ready = sem("pos_ready")
        q_blk_loaded = sem("q_blk_loaded")
        qn_ready = sem("qn_ready")
        q_diag_ready = sem("q_diag_ready")
        queried = sem("queried")
        res_loaded = sem("res_loaded")
        res_added = sem("res_added")
        res_stored = sem("res_stored")

        x_v = x.rearrange("b c y z -> c b (y z)")
        e_v = E.rearrange("n (p j) k -> p n (j k)", j=J)
        x_q = x.rearrange("b (h v) y z -> v (b h) (y z)", v=V)
        out_q = out.rearrange("b (h v) y z -> v (b h) (y z)", v=V)
        q_dram_v = q_dram.rearrange("c p a f -> p c (a f)")

        block = ctx.enter_context(nc.Block())

        @block.sync
        def _(sp):
            def load_x(b, i):
                sp.dma_start(x_in[:, i, :], x_v[:, bass.ds(b, 1), :]).then_inc(x_loaded[i], 16)

            def held(value):
                return value if isinstance(value, int) else sp.snap(value)

            def load_e(n, slot):
                for h in range(2):
                    sp.dma_start(e_nat[:, slot, h * TN:(h + 1) * TN],
                                 e_v[:, bass.ds(n[h], TN), :]).then_inc(e_loaded[slot], 16)

            def load_q(at, to):
                for h in range(2):
                    sp.dma_start(q_in_blk[:, bass.ds(to + h * (BT // 2), BT // 2), :],
                                 q_dram_v[:, bass.ds(at + h * (BT // 2), BT // 2), :]).then_inc(q_blk_loaded, 16)

            def load_res(at, col):
                for a in range(A):
                    sp.dma_start(res[a * V:(a + 1) * V, :, bass.ds(col, BN)],
                                 x_q[:, a * G * NH:(a + 1) * G * NH, bass.ds(at, BN)]).then_inc(res_loaded, 16)

            def store_res(at, col):
                for a in range(A):
                    sp.dma_start(out_q[:, a * G * NH:(a + 1) * G * NH, bass.ds(at, BN)],
                                 res[a * V:(a + 1) * V, :, bass.ds(col, BN)]).then_inc(res_stored, 16)

            def store_q(a, slot):
                sp.wait_ge(proj_read, 8 * a + 8)
                sp.dma_start(q_dram[:, :, bass.ds(a, 1), :],
                             q_nat[:, slot].rearrange("p j k g h -> p (j k) (g h)")).then_inc(q_stored[slot], 16)

            for i in range(GB):
                load_x(i, i)
            sp.dma_start(w_rows[0:QC, :], Wq).then_inc(weights_loaded, 16)
            sp.dma_start(w_rows[QC:QC + KC, :], Wk).then_inc(weights_loaded, 16)
            sp.dma_start(w_rows[QC + KC:PC, :], Wv).then_inc(weights_loaded, 16)
            for i in range(GB, 2 * GB):
                load_x(i, i)
            sp.dma_start(gam_v[:, :], gamma_v.rearrange("(p j) -> p j", j=J)).then_inc(params_loaded, 16)
            sp.dma_start(bet_v[:, :], beta_v.rearrange("(p j) -> p j", j=J)).then_inc(params_loaded, 16)
            for n in range(TN):
                sp.dma_start(gam_q[n * KD:(n + 1) * KD, :], gamma_q.rearrange("(k a) -> k a", a=1)).then_inc(params_loaded, 16)
                sp.dma_start(bet_q[n * KD:(n + 1) * KD, :], beta_q.rearrange("(k a) -> k a", a=1)).then_inc(params_loaded, 16)
            for a in range(A):
                if a < A - 1:
                    for i in range(G):
                        sp.wait_ge(x_transposed, 8 * a + i + 1)
                        load_x(8 * (a + 1) + i, i)
                else:
                    load_e((0, TN), 0)
                    load_e((2 * TN, 3 * TN), 1)
                store_q(a, a % 2)
            sp.wait_ge(q_stored[0], 16 * (A // 2))
            sp.wait_ge(q_stored[1], 16 * (A // 2))
            sp.wait_ge(q_stats_done, A)
            load_q(0, 0)
            sp.wait_ge(lam_summed, 1)
            load_res(0, 0)

            def e_pair(p, slot):
                n = held(p * 2 * TN), held(p * 2 * TN + TN)
                sp.wait_ge(e_lo_ready, 2 * p - 2)
                load_e(n, slot)

            def loads_of_block(blk):
                first, last = isinstance(blk, int) and blk == 0, isinstance(blk, int) and blk == BLOCKS - 1
                if not first:
                    before, col = held((blk - 1) * BN), held(((blk + 1) % 2) * BN)
                if not last:
                    after, to = held((blk + 1) * BN), held(((blk + 1) % 2) * BN)
                    q_at, q_to = held((blk + 1) * BT), held(((blk + 1) % 2) * BT)
                for p in range(2, PPB + 2):
                    if last and last_pair(p):
                        return
                    e_pair(blk * PPB + p, p % 2)
                    if p == 3 and not first:
                        sp.wait_ge(res_added, blk * BT)
                        store_res(before, col)
                    if p == PPB and not last:
                        sp.wait_ge(qn_ready, blk * BT + (BT - 3))
                        load_q(q_at, q_to)
                if not first:
                    sp.wait_ge(res_stored, blk * (16 * A))
                sp.wait_ge(res_added, blk * BT + (BT - 3))
                load_res(after, to)

            def last_pair(p):
                return (BLOCKS - 1) * PPB + p >= PAIRS

            loads_of_block(0)
            with sp.Fori(1, BLOCKS - 1) as blk:
                loads_of_block(blk)
            loads_of_block(BLOCKS - 1)
            last = BLOCKS - 1
            sp.wait_ge(res_added, TILES)
            store_res(last * BN, last % 2 * BN)
            sp.wait_ge(res_stored, BLOCKS * 16 * A)

        @block.gpsimd
        def _(pool):
            pool.memset(ident[:], 0.0).then_inc(memsets, 1)
            pool.memset(group_avg[:], 1.0 / GN_C).then_inc(memsets, 1)
            pool.memset(row_mask[:], 1.0).then_inc(memsets, 1)
            pool.memset(ones[:], 1.0).then_inc(consts, 1)
            pool.memset(inv_p[:], 1.0 / P).then_inc(consts, 1)
            pool.memset(eps_t[:], EPS).then_inc(consts, 1)
            pool.wait_ge(memsets, 3)
            pool.affine_select(out=ident[:], in_=ident[:], compare_op=ALU.not_equal, fill=1.0, base=0,
                               pattern=[[-1, P]], channel_multiplier=1).then_inc(consts, 1)
            avg_v = group_avg[:].rearrange("p (g i) -> p g i", i=GN_C)
            pool.affine_select(out=avg_v, in_=avg_v, compare_op=ALU.is_ge, fill=0.0, base=0,
                               pattern=[[-GN_C, C // GN_C], [0, GN_C]], channel_multiplier=1).then_inc(memsets, 1)
            pool.affine_select(out=row_mask[:], in_=row_mask[:], compare_op=ALU.is_ge, fill=0.0, base=0,
                               pattern=[[-KD, TN]], channel_multiplier=1).then_inc(memsets, 1)
            pool.wait_ge(memsets, 5)
            pool.affine_select(out=avg_v, in_=avg_v, compare_op=ALU.is_ge, fill=0.0, base=GN_C - 1,
                               pattern=[[GN_C, C // GN_C], [0, GN_C]], channel_multiplier=-1).then_inc(consts, 1)
            pool.affine_select(out=row_mask[:], in_=row_mask[:], compare_op=ALU.is_ge, fill=0.0, base=KD - 1,
                               pattern=[[KD, TN]], channel_multiplier=-1).then_inc(consts, 1)

            def norm_images(grp, par):
                pool.wait_ge(gn_ready, grp + 1)
                for i in range(GB):
                    xi = x_in[:, par * GB + i, :]
                    pool.tensor_scalar(xi, xi, gn_rstd[:, par, i:i + 1], gn_bias[:, par, i:i + 1],
                                       ALU.mult, ALU.add).then_inc(x_normed, 1)

            for grp in range(B // GB):
                norm_images(grp, grp % 2)

            pool.wait_ge(v_affine, 1)
            for j in range(J):
                vj = v_nat[:, j].rearrange("p g a v -> p (g a v)")
                pool.tensor_scalar(vj, vj, v_scale[:, j:j + 1], v_shift[:, j:j + 1],
                                   ALU.mult, ALU.add).then_inc(v_normed, 1)
            pool.wait_ge(key_max_ready, 1)
            pool.partition_all_reduce(key_top[:], key_max[:], P, RMAX).then_inc(key_top_ready, 1)

            def diag(t, slot):
                pool.wait_ge(qn_ready, t + 1)
                pool.tensor_tensor(q_diag[:, slot].rearrange("p (q n) -> p q n", n=TN),
                                   qn[:, slot].unsqueeze(2).to_broadcast([P, BH, TN]),
                                   row_mask[:].unsqueeze(1).to_broadcast([P, BH, TN]),
                                   ALU.mult).then_inc(q_diag_ready, 1)

            for i in range(2):
                pool.wait_ge(q_stored[i], 16 * (A // 2))
            diag(0, 0)
            diag(1, 1)
            with pool.Fori(1, TILES // 2) as p:
                for i in range(2):
                    pool.wait_ge(queried, 2 * p + i - 1)
                    diag(2 * p + i, i)

        @block.scalar
        def _(act):
            act.wait_ge(w_transposed, 1)
            nc.scalar.activation(w_cols[:], ps_a[:, 0, 0:PC], ACT.Copy).then_inc(w_ready, 1)

            def gn_sqrt(grp, par):
                act.wait_ge(gn_var_ready, grp + 1)
                nc.scalar.activation(gn_std[:, par], gn_var[:, par], ACT.Sqrt, bias=eps_t[:]).then_inc(gn_std_ready, 1)

            def read_xt(b, i, first):
                act.wait_ge(x_transposed, b + 1)
                if not (first and i < 2):
                    act.wait_ge(projected, b - 1)
                nc.scalar.activation(x_t[:, i % 2], ps_a[:, i % 2], ACT.Copy).then_inc(xt_ready, 1)

            def read_proj(b, a, i, slot):
                act.wait_ge(projected, b + 1)
                pr = ps_b[:, i % 2].rearrange("p (j f) -> p j f", f=P)
                nc.scalar.activation(v_nat[:, :, i, bass.ds(a, 1), :].rearrange("p j a v -> p j (a v)"),
                                     pr[:, :, QC + KC:PC], ACT.Copy)
                nc.scalar.activation(keys[:, :, i, bass.ds(a, 1), :].rearrange("p j a v -> p j (a v)"),
                                     pr[:, :, QC:QC + KC], ACT.Copy)
                nc.scalar.activation(q_nat[:, slot, :, :, i, :],
                                     pr[:, :, 0:QC].rearrange("p j (k h) -> p j k h", h=NH),
                                     ACT.Copy).then_inc(proj_read, 1)

            act.wait_ge(consts, 3)
            gn_sqrt(0, 0)
            for a in range(A):
                if a >= 2:
                    act.wait_ge(q_stored[a % 2], 16 * (a // 2))
                    act.wait_ge(q_stats_done, a - 1)
                for i in range(G):
                    read_xt(8 * a + i, i, a == 0)
                    if i > 0 or a > 0:
                        if i > 0:
                            read_proj(8 * a + i - 1, a, i - 1, a % 2)
                    if i == 1:
                        gn_sqrt(2 * a + 1, 1)
                    if i == 5 and a < A - 1:
                        gn_sqrt(2 * a + 2, 0)
                read_proj(8 * a + G - 1, a, G - 1, a % 2)

            def split_hi(t, slot, off, k):
                nc.scalar.activation(e_hi[:, slot],
                                     e_nat[:, k, off * TN:(off + 1) * TN, :].rearrange("p n (j k) -> p j n k", j=J),
                                     ACT.Copy).then_inc(e_hi_ready, 1)

            act.wait_ge(e_loaded[0], 32)
            split_hi(0, 0, 0, 0)
            split_hi(1, 1, 1, 0)
            act.wait_ge(v_var_ready, 1)
            nc.scalar.activation(v_std[:], v_mv[:, :, 1], ACT.Sqrt, bias=eps_t[:]).then_inc(v_std_ready, 1)
            for j in range(J):
                act.wait_ge(v_normed, j + 1)
                nc.scalar.activation(v_hi[:, j], v_nat[:, j].rearrange("p g a v -> p (g a v)"),
                                     ACT.Copy).then_inc(v_hi_ready, 1)
            act.wait_ge(q_var_ready, 1)
            nc.scalar.activation(q_tmp[:, 1:2], q_tmp[:, 0:1], ACT.Sqrt, bias=eps_t[:]).then_inc(q_std_ready, 1)
            for j in range(J):
                kj = keys[:, j].rearrange("p g a k -> p (g a k)")
                act.wait_ge(keys_shifted, j + 1)
                nc.scalar.activation(kj, kj, ACT.Exp).then_inc(keys_exp, 1)

            def norm_q(t, slot, off):
                nc.scalar.activation(qn[:, slot].rearrange("p (g a h) -> p g a h", g=G, a=A),
                                     q_in_blk[:, bass.ds(off, 1), :].rearrange("p o (a g h) -> p (o g) a h", g=G, a=A),
                                     ACT.Identity, bias=q_shift[:], scale=q_scale[:]).then_inc(qn_ready, 1)

            act.wait_ge(q_affine, 1)
            act.wait_ge(q_blk_loaded, 32)
            norm_q(0, 0, 0)
            norm_q(1, 1, 1)
            act.wait_ge(q_diag_ready, 1)
            norm_q(2, 0, 2)
            act.wait_ge(q_diag_ready, 2)
            norm_q(3, 1, 3)

            def tile_step(t, i, queries=True):
                pair_slot = (i // 2 + 1) % 2
                if i % 2 == 0:
                    act.wait_ge(e_loaded[pair_slot], (t // 4 + 1) * 32)
                act.wait_ge(pos_summed, t - 1)
                split_hi(t, i % 2, i % 2, pair_slot)
                if queries:
                    if i == 0:
                        act.wait_ge(q_blk_loaded, ((t + 2) // BT + 1) * 32)
                    act.wait_ge(q_diag_ready, t + 1)
                    norm_q(t + 2, i % 2, (t + 2) % (2 * BT))

            with act.Fori(0, TILES // 4 - 1) as q:
                for i in range(4):
                    tile_step(4 * q + 2 + i, i)
            tile_step(TILES - 2, 0, queries=False)
            tile_step(TILES - 1, 1, queries=False)

        @block.vector
        def _(dve):
            steps = [0]

            def link(ins):
                steps[0] += 1
                ins.then_inc(dve_step, 1)
                dve.wait_ge(dve_step, steps[0])

            dve.wait_ge(consts, 6)
            link(nc.vector.tensor_reduce(fold[:], ident[:].rearrange("p (m k) -> p k m", k=KD), AX.X, ALU.add))
            nc.vector.tensor_copy(same_k[:].rearrange("p (m k) -> p m k", k=KD),
                                  fold[:].unsqueeze(1).to_broadcast([P, TN, KD])).then_inc(same_k_ready, 1)

            def gn_moments(grp, par):
                for i in range(GB):
                    s = par * GB + i
                    dve.wait_ge(x_loaded[s], 16 * (grp // 2 + 1))
                    for half in range(2):
                        ins = nc.vector.bn_stats(bn6[:, s, half], x_in[:, s, half * BANK:(half + 1) * BANK])
                    if i == GB - 1:
                        link(ins)
                for i in range(GB):
                    s = par * GB + i
                    ins = nc.vector.bn_aggr(mv[:, par, i], bn6[:, s].rearrange("p a s -> p (a s)"))
                link(ins)
                link(nc.vector.tensor_tensor(gn_sq[:, par], mv[:, par, :, 0], mv[:, par, :, 0], ALU.mult))
                nc.vector.tensor_copy(gn_in[:, par, :, 0], mv[:, par, :, 0])
                nc.vector.tensor_tensor(gn_in[:, par, :, 1], gn_sq[:, par], mv[:, par, :, 1], ALU.add).then_inc(gn_stats, 1)

            def gn_finish(grp, par):
                dve.wait_ge(gn_summed, grp + 1)
                nc.vector.tensor_copy(gn_out[:, par].rearrange("p b s -> p (b s)"), gn_ps).then_inc(gn_read, 1)
                dve.wait_ge(gn_read, grp + 1)
                link(nc.vector.tensor_tensor(gn_sq[:, par], gn_out[:, par, :, 0], gn_out[:, par, :, 0], ALU.mult))
                nc.vector.tensor_tensor(gn_var[:, par], gn_out[:, par, :, 1], gn_sq[:, par], ALU.subtract).then_inc(gn_var_ready, 1)
                dve.wait_ge(gn_std_ready, grp + 1)
                link(nc.vector.reciprocal(gn_rstd[:, par], gn_std[:, par]))
                nc.vector.scalar_tensor_tensor(gn_bias[:, par], gn_out[:, par, :, 0], -1.0, gn_rstd[:, par],
                                               ALU.mult, ALU.mult).then_inc(gn_ready, 1)

            def qv_stats(a, slot):
                dve.wait_ge(proj_read, 8 * a + 8)
                for k in range(KD):
                    ins = nc.vector.bn_stats(q_stats[:, k, a], q_nat[:, slot, :, k].rearrange("p j g h -> p j (g h)"))
                ins.then_inc(q_stats_done, 1)
                for j in range(J):
                    ins = nc.vector.bn_stats(v_stats[:, j, a], v_nat[:, j, :, a, :])
                return ins

            gn_moments(0, 0)
            gn_finish(0, 0)
            for a in range(A):
                gn_moments(2 * a + 1, 1)
                gn_finish(2 * a + 1, 1)
                if a > 0:
                    qv_stats(a - 1, (a - 1) % 2)
                if a < A - 1:
                    gn_moments(2 * a + 2, 0)
                    gn_finish(2 * a + 2, 0)
            link(qv_stats(A - 1, (A - 1) % 2))

            for j in range(J):
                ins = nc.vector.bn_aggr(v_mv[:, j], v_stats[:, j].rearrange("p a s -> p (a s)"))
            ins.then_inc(v_var_ready, 1)
            dve.wait_ge(v_std_ready, 1)
            dve.wait_ge(params_loaded, 16 * (2 + 2 * TN))
            link(nc.vector.reciprocal(v_tmp[:], v_std[:]))
            link(nc.vector.tensor_tensor(v_scale[:], v_tmp[:], gam_v[:], ALU.mult))
            link(nc.vector.tensor_tensor(v_tmp[:], v_mv[:, :, 0], v_scale[:], ALU.mult))
            nc.vector.tensor_tensor(v_shift[:], bet_v[:], v_tmp[:], ALU.subtract).then_inc(v_affine, 1)

            for k in range(KD):
                ins = nc.vector.bn_aggr(q_mv[:, k], q_stats[:, k].rearrange("p a s -> p (a s)"))
            link(ins)
            link(nc.vector.tensor_tensor(q_sq[:], q_mv[:, :, 0], q_mv[:, :, 0], ALU.mult))
            link(nc.vector.tensor_tensor(q_sq[:], q_sq[:], q_mv[:, :, 1], ALU.add))
            nc.vector.tensor_copy(q_in[:, 0], q_mv[:, :, 0].unsqueeze(1).to_broadcast([P, TN, KD]))
            nc.vector.tensor_copy(q_in[:, 1], q_sq[:].unsqueeze(1).to_broadcast([P, TN, KD])).then_inc(q_moments, 1)

            def split_lo(slot, off, k, t):
                dve.wait_ge(e_hi_ready, t + 1)
                nc.vector.tensor_tensor(e_lo[:, slot],
                                        e_nat[:, k, off * TN:(off + 1) * TN, :].rearrange("p n (j k) -> p j n k", j=J),
                                        e_hi[:, slot].bitcast(f32), ALU.subtract).then_inc(e_lo_ready, 1)

            split_lo(0, 0, 0, 0)
            for j in range(J):
                dve.wait_ge(v_hi_ready, j + 1)
                nc.vector.tensor_tensor(v_lo[:, j], v_nat[:, j].rearrange("p g a v -> p (g a v)"),
                                        v_hi[:, j].bitcast(f32), ALU.subtract).then_inc(v_lo_ready, 1)
            split_lo(1, 1, 0, 1)

            nc.vector.tensor_reduce(key_max[:], keys[:].rearrange("p j g a k -> p (g a k) j"), AX.X,
                                    ALU.max).then_inc(key_max_ready, 1)
            dve.wait_ge(q_averaged, 1)
            link(nc.vector.tensor_copy(q_out[:], ps_b[:, 1, 0:2]))
            link(nc.vector.tensor_tensor(q_tmp[:, 2:3], q_out[:, 0:1], q_out[:, 0:1], ALU.mult))
            nc.vector.tensor_tensor(q_tmp[:, 0:1], q_out[:, 1:2], q_tmp[:, 2:3], ALU.subtract).then_inc(q_var_ready, 1)
            dve.wait_ge(q_std_ready, 1)
            link(nc.vector.reciprocal(q_tmp[:, 2:3], q_tmp[:, 1:2]))
            link(nc.vector.tensor_tensor(q_scale[:], q_tmp[:, 2:3], gam_q[:], ALU.mult))
            link(nc.vector.tensor_tensor(q_tmp[:, 3:4], q_out[:, 0:1], q_scale[:], ALU.mult))
            nc.vector.tensor_tensor(q_shift[:], bet_q[:], q_tmp[:, 3:4], ALU.subtract).then_inc(q_affine, 1)
            dve.wait_ge(key_top_ready, 1)
            for j in range(J):
                kj = keys[:, j].rearrange("p g a k -> p (g a k)")
                nc.vector.tensor_tensor(kj, kj, key_top[:], ALU.subtract).then_inc(keys_shifted, 1)
            dve.wait_ge(keys_exp, J)
            nc.vector.tensor_reduce(exp_sum[:], keys[:].rearrange("p j g a k -> p (g a k) j"), AX.X,
                                    ALU.add).then_inc(exp_summed, 1)
            dve.wait_ge(lam_summed, 1)
            link(nc.vector.reciprocal(inv_sum[:], ps_b[:, 1, 0:B // TN]))
            for s in range(B // TN):
                nc.vector.scalar_tensor_tensor(
                    lam_diag[:, s * TN * V:(s + 1) * TN * V].rearrange("p (b v) -> p b v", v=V),
                    ps_b[:, 0, s * TN * V:(s + 1) * TN * V].rearrange("p (b v) -> p b v", v=V),
                    inv_sum[:, s:s + 1], row_mask[:].unsqueeze(2).to_broadcast([P, TN, V]),
                    ALU.mult, ALU.mult).then_inc(lam_masked, 1)
            dve.wait_ge(lam_spread, 1)
            link(nc.vector.tensor_copy(content[:], ps_b[:, 1]))

            def read_pos(t, slot):
                dve.wait_ge(pos_summed, t + 1)
                nc.vector.tensor_tensor(pos[:, slot], ps_a[:, slot], content[:], ALU.add).then_inc(pos_ready, 1)

            def add_out(t, slot, off):
                dve.wait_ge(queried, t + 1)
                for a in range(A):
                    rows = slice(a * V, (a + 1) * V)
                    r = res[rows, :, bass.ds(off, TN)].rearrange("v (g h) n -> v g h n", h=NH)
                    ins = nc.vector.tensor_tensor(
                        r, ps_b[rows, slot].rearrange("v (g a h n) -> v g a h n", g=G, a=A, h=NH)[:, :, a],
                        r, ALU.add)
                ins.then_inc(res_added, 1)

            for i in range(2):
                dve.wait_ge(q_stored[i], 16 * (A // 2))
            read_pos(0, 0)
            split_lo(0, 0, 1, 2)

            def tile_step(q, i, lo=True):
                t = 4 * q + 1 + i
                read_pos(t, (i + 1) % 2)
                if lo:
                    split_lo((i + 1) % 2, (i + 1) % 2, ((i + 3) // 2) % 2, t + 2)
                if i == 0:
                    dve.wait_ge(res_loaded, (q // (BT // 4) + 1) * (16 * A))
                add_out(t - 1, i % 2, (q % (BT // 2)) * (4 * TN) + i * TN)

            with dve.Fori(0, TILES // 4 - 1) as q:
                for i in range(4):
                    tile_step(q, i)
            for i in range(3):
                tile_step(TILES // 4 - 1, i, lo=i < 1)
            add_out(TILES - 1, 1, 2 * BN - TN)

        @block.tensor
        def _(pe):
            pe.wait_ge(consts, 4)
            pe.wait_ge(weights_loaded, 16 * 3)
            nc.tensor.transpose(ps_a[:, 0, 0:PC], w_rows[:], ident[0:PC, 0:PC]).then_inc(w_transposed, 1)
            pe.wait_ge(consts, 6)

            def gn_average(grp, par, reads):
                pe.wait_ge(gn_stats, grp + 1)
                if reads:
                    pe.wait_ge(proj_read, reads)
                nc.tensor.matmul(gn_ps, group_avg[:], gn_in[:, par].rearrange("p b s -> p (b s)"),
                                 start=True, stop=True).then_inc(gn_summed, 1)

            def transpose_image(b, i):
                pe.wait_ge(x_normed, b + 1)
                if b >= 2:
                    pe.wait_ge(xt_ready, b - 1)
                for j in range(J):
                    ins = nc.tensor.transpose(ps_a[:, i % 2, j * C:(j + 1) * C], x_in[:, i, j * D:(j + 1) * D], ident[:])
                ins.then_inc(x_transposed, 1)

            def project(b, i):
                pe.wait_ge(xt_ready, b + 1)
                if i % GB == 1:
                    pe.wait_ge(gn_read, min(b // GB + 2, B // GB))
                if b >= 2:
                    pe.wait_ge(proj_read, b - 1)
                for j in range(J):
                    ins = nc.tensor.matmul(ps_b[:, i % 2, j * P:j * P + PC], x_t[:, i % 2, j * C:(j + 1) * C], w_cols[:],
                                           start=True, stop=True)
                ins.then_inc(projected, 1)

            gn_average(0, 0, 0)
            pe.wait_ge(gn_read, 1)
            pe.wait_ge(w_ready, 1)
            for a in range(A):
                for i in range(G):
                    b = 8 * a + i
                    transpose_image(b, i)
                    if b > 0:
                        project(b - 1, (i - 1) % G)
                    if i == 1:
                        gn_average(2 * a + 1, 1, b - 1)
                    if i == 5 and a < A - 1:
                        gn_average(2 * a + 2, 0, b - 1)
            project(B - 1, G - 1)

            def sum_tile(t, slot, first=False):
                pe.wait_ge(e_hi_ready, t + 1)
                pe.wait_ge(e_lo_ready, t + 1)
                for j in range(J):
                    if first:
                        pe.wait_ge(v_lo_ready, j + 1)
                    for n, (e, v) in enumerate(((e_hi, v_hi), (e_hi, v_lo), (e_lo, v_hi))):
                        for half in range(BV // BANK):
                            cols = slice(half * BANK, (half + 1) * BANK)
                            ins = nc.tensor.matmul(ps_a[:, slot, cols], e[:, slot, j].rearrange("p n k -> p (n k)"),
                                                   v[:, j, cols], start=(j == 0 and n == 0), stop=(j == J - 1 and n == 2))
                ins.then_inc(pos_summed, 1)

            def query_tile(t, slot):
                pe.wait_ge(pos_ready, t + 1)
                pe.wait_ge(q_diag_ready, t + 1)
                for g in range(G):
                    cols = slice(g * P, (g + 1) * P)
                    ins = nc.tensor.matmul(ps_b[:, slot, cols], pos[:, slot, cols], q_diag[:, slot, cols],
                                           start=True, stop=True)
                ins.then_inc(queried, 1)

            pe.wait_ge(proj_read, B)
            sum_tile(0, 0, first=True)
            pe.wait_ge(q_moments, 1)
            for s in range(2):
                ins = nc.tensor.matmul(ps_b[:, 1, s:s + 1], q_in[:, s].rearrange("p n k -> p (n k)"), inv_p[:],
                                       start=True, stop=True)
            ins.then_inc(q_averaged, 1)
            sum_tile(1, 1)
            pe.wait_ge(keys_exp, J)
            for s in range(B // TN):
                gs = TN // A
                for j in range(J):
                    nc.tensor.matmul(ps_b[:, 0, s * TN * V:(s + 1) * TN * V],
                                     keys[:, j, s * gs:(s + 1) * gs].rearrange("p g a k -> p (g a k)"),
                                     v_nat[:, j, s * gs:(s + 1) * gs].rearrange("p g a v -> p (g a v)"),
                                     start=(j == 0), stop=(j == J - 1))
            pe.wait_ge(exp_summed, 1)
            pe.wait_ge(q_var_ready, 1)
            for s in range(B // TN):
                ins = nc.tensor.matmul(ps_b[:, 1, s:s + 1], exp_sum[:, s * P:(s + 1) * P], ones[:], start=True, stop=True)
            ins.then_inc(lam_summed, 1)
            pe.wait_ge(same_k_ready, 1)
            for s in range(B // TN):
                cols = slice(s * TN * V, (s + 1) * TN * V)
                pe.wait_ge(lam_masked, B // TN)
                ins = nc.tensor.matmul(ps_b[:, 1, cols], same_k[:], lam_diag[:, cols], start=True, stop=True)
            ins.then_inc(lam_spread, 1)
            query_tile(0, 0)
            with pe.Fori(0, TILES // 4 - 1) as q:
                for i in range(4):
                    sum_tile(4 * q + 2 + i, i % 2)
                    query_tile(4 * q + 1 + i, (i + 1) % 2)
            sum_tile(TILES - 2, 0)
            query_tile(TILES - 3, 1)
            sum_tile(TILES - 1, 1)
            query_tile(TILES - 2, 0)
            query_tile(TILES - 1, 1)


_INS = ["x", "L0_conv_Wq", "L0_conv_Wk", "L0_conv_Wv", "L0_conv_E", "L0_conv_gamma_v", "L0_conv_beta_v",
        "L0_conv_gamma_q", "L0_conv_beta_q"]


def kernel(**inputs):
    import numpy as _np
    import concourse.bacc as _bacc
    from concourse import mybir as _mybir
    from concourse.bass_utils import run_bass_kernel_spmd as _run

    nc = _bacc.Bacc("TRN2", target_bir_lowering=False, num_devices=1)
    arrays, args = {}, []
    for name in _INS:
        a = _np.ascontiguousarray(inputs[name])
        arrays[f"in_{name}"] = a
        args.append(nc.dram_tensor(f"in_{name}", a.shape, _mybir.dt.from_np(a.dtype), kind="ExternalInput").ap())
    shape = arrays["in_x"].shape
    args.append(nc.dram_tensor("out_dram", shape, _mybir.dt.float32, kind="ExternalOutput").ap())
    lambda_conv_kernel(nc, *args)
    r = _run(nc, [arrays], core_ids=[0])
    return r.results[0]["out_dram"]
```

```python
import concourse.bass as bass
from concourse import mybir
from contextlib import ExitStack


def lambda_conv_kernel(nc: bass.Bass, x, Wq, Wk, Wv, E, gamma_v, beta_v, gamma_q, beta_q, out):
    f32 = mybir.dt.float32
    f32r = mybir.dt.float32r
    ALU = mybir.AluOpType
    ACT = mybir.ActivationFunctionType
    AX = mybir.AxisListType
    RMAX = bass.bass_isa.ReduceOp.max

    P = 128
    B, C, H, W = x.shape
    D = C
    J = H * W // D
    N = H * W
    KD = Wk.shape[0]
    NH = Wq.shape[0] // KD
    V = Wv.shape[0]
    A = P // V
    G = B // A
    BV = B * V
    BH = B * NH
    QC, KC = KD * NH, KD
    PC = QC + KC + V
    TN = P // KD
    TILES = N // TN
    HALF = P // 2
    BANK = 512
    BT = 16
    BLOCKS = TILES // BT
    BN = BT * TN
    PAIRS = TILES // 2
    PPB = BT // 2
    GB = 4
    QS = 3
    GN_C = C // 32
    EPS = 1e-5

    ctx = ExitStack()

    def sb(name, shape, dt=f32, stack=ctx):
        return stack.enter_context(nc.sbuf_tensor(name, shape, dt))

    with ctx:
        ident = sb("ident", [P, P])
        group_avg = sb("group_avg", [P, P])
        same_k = sb("same_k", [P, P])
        row_mask = sb("row_mask", [P, TN])
        fold = sb("fold", [P, KD])
        ones = sb("ones", [P, 1])
        inv_p = sb("inv_p", [P, 1])
        eps_t = sb("eps_t", [P, 1])
        sqrt_first = sb("sqrt_first", [P, 1])
        w_rows = sb("w_rows", [PC, D])
        w_cols = sb("w_cols", [D, PC])
        gam_v = sb("gam_v", [P, J])
        bet_v = sb("bet_v", [P, J])
        gam_q = sb("gam_q", [P, 1])
        bet_q = sb("bet_q", [P, 1])
        bn6 = sb("bn6", [P, 2 * GB, 2, 6])
        mv = sb("mv", [P, 2, GB, 2])
        gn_in = sb("gn_in", [P, 2, GB, 2])
        gn_sq = sb("gn_sq", [P, 2, GB])
        gn_out = sb("gn_out", [P, 2, GB, 2])
        gn_var = sb("gn_var", [P, 2, GB])
        gn_std = sb("gn_std", [P, 2, GB])
        gn_rstd = sb("gn_rstd", [P, 2, GB])
        gn_bias = sb("gn_bias", [P, 2, GB])
        v_stats = sb("v_stats", [P, J, A, 6])
        q_stats = sb("q_stats", [P, KD, A, 6])
        v_mv = sb("v_mv", [P, J, 2])
        v_std = sb("v_std", [P, J])
        v_scale = sb("v_scale", [P, J])
        v_tmp = sb("v_tmp", [P, J])
        v_shift = sb("v_shift", [P, J])
        q_mv = sb("q_mv", [P, KD, 2])
        q_in = sb("q_in", [P, 2, TN, KD])
        q_sq = sb("q_sq", [P, KD])
        q_out = sb("q_out", [P, 2])
        q_tmp = sb("q_tmp", [P, 4])
        q_scale = sb("q_scale", [P, 1])
        q_shift = sb("q_shift", [P, 1])
        key_max = sb("key_max", [P, B * KD])
        key_top = sb("key_top", [P, B * KD])
        exp_sum = sb("exp_sum", [P, B * KD])
        inv_sum = sb("inv_sum", [P, B // TN])
        qn = sb("qn", [P, 2, BH])
        e_nat = sb("e_nat", [P, 2, 2 * TN, J * KD])
        e_hi = sb("e_hi", [P, 2, J, TN, KD], f32r)
        e_lo = sb("e_lo", [P, 2, J, TN, KD], f32r)

        keys = sb("keys", [P, J, G, A, KD])
        early = ExitStack()
        x_in = sb("x_in", [P, 2 * GB, J * D], stack=early)
        x_t = sb("x_t", [D, 2, J * C], stack=early)
        early.close()
        v_hi = sb("v_hi", [P, J, BV], f32r)
        v_lo = sb("v_lo", [P, J, BV], f32r)
        early = ExitStack()
        q_nat = sb("q_nat", [P, QS, J, KD, G, NH], stack=early)
        v_nat = sb("v_nat", [P, J, G, A, V], stack=early)
        early.close()
        q_in_blk = sb("q_in_blk", [P, 2 * BT, BH])
        pos = sb("pos", [P, 2, BV])
        q_diag = sb("q_diag", [P, 2, B * NH * TN])
        lam_diag = sb("lam_diag", [P, BV])
        content = sb("content", [P, BV])
        res = sb("res", [P, G * NH, 2 * BN])

        ps_a = ctx.enter_context(nc.psum_tensor("ps_a", [P, 2, BV], f32))
        ps_b = ctx.enter_context(nc.psum_tensor("ps_b", [P, 2, BV], f32))
        q_dram = nc.dram_tensor("q_dram", (C, A, J * KD, G * NH), f32).ap()
        q_ps = ps_b[:, 1, BANK:BANK + 2]
        gn_ps = ps_b[:, 0, 0:2 * GB]

        def sem(name):
            return ctx.enter_context(nc.semaphore(name))

        x_loaded = [sem(f"x_loaded{i}") for i in range(2 * GB)]
        weights_loaded = sem("weights_loaded")
        params_loaded = sem("params_loaded")
        memsets = sem("memsets")
        consts = sem("consts")
        w_transposed = sem("w_transposed")
        w_ready = sem("w_ready")
        same_k_ready = sem("same_k_ready")
        gn_stats = sem("gn_stats")
        gn_summed = sem("gn_summed")
        gn_read = sem("gn_read")
        gn_var_ready = sem("gn_var_ready")
        gn_std_ready = sem("gn_std_ready")
        gn_ready = sem("gn_ready")
        x_normed = sem("x_normed")
        x_transposed = sem("x_transposed")
        xt_ready = sem("xt_ready")
        projected = sem("projected")
        proj_read = sem("proj_read")
        q_stats_done = sem("q_stats_done")
        q_stored = [sem(f"q_stored{i}") for i in range(QS)]
        dve_step = sem("dve_step")
        v_var_ready = sem("v_var_ready")
        v_std_ready = sem("v_std_ready")
        v_affine = sem("v_affine")
        v_normed = sem("v_normed")
        v_hi_ready = sem("v_hi_ready")
        v_lo_ready = sem("v_lo_ready")
        key_max_ready = sem("key_max_ready")
        key_top_ready = sem("key_top_ready")
        keys_shifted = sem("keys_shifted")
        keys_exp = sem("keys_exp")
        exp_summed = sem("exp_summed")
        q_moments = sem("q_moments")
        q_averaged = sem("q_averaged")
        q_var_ready = sem("q_var_ready")
        q_std_ready = sem("q_std_ready")
        q_affine = sem("q_affine")
        lam_summed = sem("lam_summed")
        lam_zeroed = sem("lam_zeroed")
        lam_masked = sem("lam_masked")
        lam_spread = sem("lam_spread")
        e_loaded = [sem(f"e_loaded{i}") for i in range(2)]
        e_hi_ready = sem("e_hi_ready")
        e_lo_ready = sem("e_lo_ready")
        pos_summed = sem("pos_summed")
        pos_copied = sem("pos_copied")
        pos_ready = sem("pos_ready")
        pool_step = sem("pool_step")
        q_blk_loaded = sem("q_blk_loaded")
        qn_ready = sem("qn_ready")
        q_diag_ready = sem("q_diag_ready")
        queried = sem("queried")
        res_loaded = sem("res_loaded")
        res_added = sem("res_added")
        res_stored = sem("res_stored")

        x_v = x.rearrange("b c y z -> c b (y z)")
        e_v = E.rearrange("n (p j) k -> p n (j k)", j=J)
        x_q = x.rearrange("b (h v) y z -> v (b h) (y z)", v=V)
        out_q = out.rearrange("b (h v) y z -> v (b h) (y z)", v=V)
        q_dram_v = q_dram.rearrange("c a p f -> p (c a) f")

        block = ctx.enter_context(nc.Block())

        @block.sync
        def _(sp):
            def load_x(b, i):
                sp.dma_start(x_in[:, i, :], x_v[:, bass.ds(b, 1), :]).then_inc(x_loaded[i], 16)

            def held(value):
                return value if isinstance(value, int) else sp.snap(value)

            def load_e(n, slot):
                for h in range(2):
                    sp.dma_start(e_nat[:, slot, h * TN:(h + 1) * TN],
                                 e_v[:, bass.ds(n[h], TN), :]).then_inc(e_loaded[slot], 16)

            def load_q(at, to):
                for h in range(2):
                    rows = BT // 2
                    sp.dma_start(q_in_blk[:, bass.ds(to + h * rows, rows), :].rearrange("p c (a f) -> p (c a) f", a=A),
                                 q_dram_v[:, bass.ds((at + h * rows) * A, rows * A), :]).then_inc(q_blk_loaded, 16)

            def load_res(at, col):
                for a in range(A):
                    sp.dma_start(res[a * V:(a + 1) * V, :, bass.ds(col, BN)],
                                 x_q[:, a * G * NH:(a + 1) * G * NH, bass.ds(at, BN)]).then_inc(res_loaded, 16)

            def store_res(at, col):
                for a in range(A):
                    sp.dma_start(out_q[:, a * G * NH:(a + 1) * G * NH, bass.ds(at, BN)],
                                 res[a * V:(a + 1) * V, :, bass.ds(col, BN)]).then_inc(res_stored, 16)

            def store_q(a):
                sp.wait_ge(proj_read, 8 * a + 8)
                sp.dma_start(q_dram[:, a], q_nat[:, a % QS].rearrange("p j k g h -> p (j k) (g h)")
                             ).then_inc(q_stored[a % QS], 16)

            for i in range(GB):
                load_x(i, i)
            sp.dma_start(w_rows[0:QC, :], Wq).then_inc(weights_loaded, 16)
            sp.dma_start(w_rows[QC:QC + KC, :], Wk).then_inc(weights_loaded, 16)
            sp.dma_start(w_rows[QC + KC:PC, :], Wv).then_inc(weights_loaded, 16)
            for i in range(GB, 2 * GB):
                load_x(i, i)
            sp.dma_start(gam_v[:, :], gamma_v.rearrange("(p j) -> p j", j=J)).then_inc(params_loaded, 16)
            sp.dma_start(bet_v[:, :], beta_v.rearrange("(p j) -> p j", j=J)).then_inc(params_loaded, 16)
            for n in range(TN):
                sp.dma_start(gam_q[n * KD:(n + 1) * KD, :], gamma_q.rearrange("(k a) -> k a", a=1)).then_inc(params_loaded, 16)
                sp.dma_start(bet_q[n * KD:(n + 1) * KD, :], beta_q.rearrange("(k a) -> k a", a=1)).then_inc(params_loaded, 16)
            for a in range(A - 1):
                for i in range(G):
                    sp.wait_ge(x_transposed, 8 * a + i + 1)
                    load_x(8 * (a + 1) + i, i)
                    if a > 0 and i == 2:
                        store_q(a - 1)
            load_e((0, TN), 0)
            load_e((2 * TN, 3 * TN), 1)
            store_q(A - 2)
            store_q(A - 1)
            for i in range(QS):
                sp.wait_ge(q_stored[i], 16 * len(range(i, A, QS)))
            sp.wait_ge(q_stats_done, A)
            load_q(0, 0)
            sp.wait_ge(lam_summed, 1)
            load_res(0, 0)

            def e_pair(p, slot):
                n = held(p * 2 * TN), held(p * 2 * TN + TN)
                sp.wait_ge(e_lo_ready, 2 * p - 2)
                load_e(n, slot)

            def loads_of_block(blk):
                first, last = isinstance(blk, int) and blk == 0, isinstance(blk, int) and blk == BLOCKS - 1
                if not first:
                    before, col = held((blk - 1) * BN), held(((blk + 1) % 2) * BN)
                if not last:
                    after, to = held((blk + 1) * BN), held(((blk + 1) % 2) * BN)
                    q_at, q_to = held((blk + 1) * BT), held(((blk + 1) % 2) * BT)
                for p in range(2, PPB + 2):
                    if last and last_pair(p):
                        return
                    e_pair(blk * PPB + p, p % 2)
                    if p == 3 and not first:
                        sp.wait_ge(res_added, blk * BT)
                        store_res(before, col)
                    if p == PPB and not last:
                        sp.wait_ge(qn_ready, blk * BT + (BT - 3))
                        load_q(q_at, q_to)
                if not first:
                    sp.wait_ge(res_stored, blk * (16 * A))
                sp.wait_ge(res_added, blk * BT + (BT - 3))
                load_res(after, to)

            def last_pair(p):
                return (BLOCKS - 1) * PPB + p >= PAIRS

            loads_of_block(0)
            with sp.Fori(1, BLOCKS - 1) as blk:
                loads_of_block(blk)
            loads_of_block(BLOCKS - 1)
            last = BLOCKS - 1
            sp.wait_ge(res_added, TILES)
            store_res(last * BN, last % 2 * BN)
            sp.wait_ge(res_stored, BLOCKS * 16 * A)

        @block.gpsimd
        def _(pool):
            pool.memset(ident[:], 0.0).then_inc(memsets, 1)
            pool.memset(group_avg[:], 1.0 / GN_C).then_inc(memsets, 1)
            pool.memset(row_mask[:], 1.0).then_inc(memsets, 1)
            pool.memset(ones[:], 1.0).then_inc(consts, 1)
            pool.memset(inv_p[:], 1.0 / P).then_inc(consts, 1)
            pool.memset(eps_t[:], EPS).then_inc(consts, 1)
            pool.wait_ge(memsets, 3)
            pool.affine_select(out=ident[:], in_=ident[:], compare_op=ALU.not_equal, fill=1.0, base=0,
                               pattern=[[-1, P]], channel_multiplier=1).then_inc(consts, 1)
            avg_v = group_avg[:].rearrange("p (g i) -> p g i", i=GN_C)
            pool.affine_select(out=avg_v, in_=avg_v, compare_op=ALU.is_ge, fill=0.0, base=0,
                               pattern=[[-GN_C, C // GN_C], [0, GN_C]], channel_multiplier=1).then_inc(memsets, 1)
            pool.affine_select(out=row_mask[:], in_=row_mask[:], compare_op=ALU.is_ge, fill=0.0, base=0,
                               pattern=[[-KD, TN]], channel_multiplier=1).then_inc(memsets, 1)
            pool.wait_ge(memsets, 5)
            pool.affine_select(out=avg_v, in_=avg_v, compare_op=ALU.is_ge, fill=0.0, base=GN_C - 1,
                               pattern=[[GN_C, C // GN_C], [0, GN_C]], channel_multiplier=-1).then_inc(consts, 1)
            pool.affine_select(out=row_mask[:], in_=row_mask[:], compare_op=ALU.is_ge, fill=0.0, base=KD - 1,
                               pattern=[[KD, TN]], channel_multiplier=-1).then_inc(consts, 1)

            def norm_images(grp, par):
                pool.wait_ge(gn_ready, grp + 1)
                for i in range(GB):
                    xi = x_in[:, par * GB + i, :]
                    pool.tensor_scalar(xi, xi, gn_rstd[:, par, i:i + 1], gn_bias[:, par, i:i + 1],
                                       ALU.mult, ALU.add).then_inc(x_normed, 1)

            for grp in range(B // GB):
                norm_images(grp, grp % 2)

            pool.wait_ge(v_affine, 1)
            for j in range(J):
                vj = v_nat[:, j].rearrange("p g a v -> p (g a v)")
                pool.tensor_scalar(vj, vj, v_scale[:, j:j + 1], v_shift[:, j:j + 1],
                                   ALU.mult, ALU.add).then_inc(v_normed, 1)
            pool.wait_ge(key_max_ready, 1)
            pool.partition_all_reduce(key_top[:], key_max[:], P, RMAX).then_inc(key_top_ready, 1)
            for j in range(1, J):
                kj = keys[:, j].rearrange("p g a k -> p (g a k)")
                before = keys[:, 0].rearrange("p g a k -> p (g a k)") if j == 1 else exp_sum[:]
                pool.wait_ge(keys_exp, j + 1)
                if j > 1:
                    pool.wait_ge(pool_step, j - 1)
                pool.tensor_tensor(exp_sum[:], before, kj, ALU.add).then_inc(pool_step if j < J - 1 else exp_summed, 1)

            def diag(t, slot):
                pool.wait_ge(qn_ready, t + 1)
                pool.tensor_tensor(q_diag[:, slot].rearrange("p (q n) -> p q n", n=TN),
                                   qn[:, slot].unsqueeze(2).to_broadcast([P, BH, TN]),
                                   row_mask[:].unsqueeze(1).to_broadcast([P, BH, TN]),
                                   ALU.mult).then_inc(q_diag_ready, 1)

            for i in range(QS):
                pool.wait_ge(q_stored[i], 16 * len(range(i, A, QS)))
            pool.wait_ge(q_stats_done, A)
            pool.memset(lam_diag[:], 0.0).then_inc(lam_zeroed, 1)
            diag(0, 0)
            diag(1, 1)
            with pool.Fori(1, TILES // 2) as p:
                for i in range(2):
                    pool.wait_ge(queried, 2 * p + i - 1)
                    diag(2 * p + i, i)

        @block.scalar
        def _(act):
            act.wait_ge(consts, 3)
            nc.scalar.activation(sqrt_first[:], eps_t[:], ACT.Sqrt)
            act.wait_ge(w_transposed, 1)
            nc.scalar.activation(w_cols[:], ps_a[:, 0, 0:PC], ACT.Copy).then_inc(w_ready, 1)

            def gn_sqrt(grp, par):
                act.wait_ge(gn_var_ready, grp + 1)
                nc.scalar.activation(gn_std[:, par], gn_var[:, par], ACT.Sqrt, bias=eps_t[:]).then_inc(gn_std_ready, 1)

            def read_xt(b, i, first):
                act.wait_ge(x_transposed, b + 1)
                if not (first and i < 2):
                    act.wait_ge(projected, b - 1)
                nc.scalar.activation(x_t[:, i % 2], ps_a[:, i % 2], ACT.Copy).then_inc(xt_ready, 1)

            def read_proj(b, a, i, slot):
                act.wait_ge(projected, b + 1)
                pr = ps_b[:, i % 2].rearrange("p (j f) -> p j f", f=P)
                nc.scalar.activation(v_nat[:, :, i, bass.ds(a, 1), :].rearrange("p j a v -> p j (a v)"),
                                     pr[:, :, QC + KC:PC], ACT.Copy)
                nc.scalar.activation(keys[:, :, i, bass.ds(a, 1), :].rearrange("p j a v -> p j (a v)"),
                                     pr[:, :, QC:QC + KC], ACT.Copy)
                nc.scalar.activation(q_nat[:, slot, :, :, i, :],
                                     pr[:, :, 0:QC].rearrange("p j (k h) -> p j k h", h=NH),
                                     ACT.Copy).then_inc(proj_read, 1)

            gn_sqrt(0, 0)
            for a in range(A):
                if a >= QS:
                    act.wait_ge(q_stored[a % QS], 16 * (a // QS))
                    act.wait_ge(q_stats_done, a - QS + 1)
                for i in range(G):
                    read_xt(8 * a + i, i, a == 0)
                    if i > 0:
                        read_proj(8 * a + i - 1, a, i - 1, a % QS)
                    if i == 2:
                        gn_sqrt(2 * a + 1, 1)
                    if i == 6 and a < A - 1:
                        gn_sqrt(2 * a + 2, 0)
                read_proj(8 * a + G - 1, a, G - 1, a % QS)

            def split_hi(t, slot, off, k):
                nc.scalar.activation(e_hi[:, slot],
                                     e_nat[:, k, off * TN:(off + 1) * TN, :].rearrange("p n (j k) -> p j n k", j=J),
                                     ACT.Copy).then_inc(e_hi_ready, 1)

            act.wait_ge(e_loaded[0], 32)
            split_hi(0, 0, 0, 0)
            split_hi(1, 1, 1, 0)
            act.wait_ge(v_var_ready, 1)
            nc.scalar.activation(v_std[:], v_mv[:, :, 1], ACT.Sqrt, bias=eps_t[:]).then_inc(v_std_ready, 1)
            for j in range(J):
                act.wait_ge(v_normed, j + 1)
                nc.scalar.activation(v_hi[:, j], v_nat[:, j].rearrange("p g a v -> p (g a v)"),
                                     ACT.Copy).then_inc(v_hi_ready, 1)

            def copy_pos(t):
                act.wait_ge(pos_summed, t + 1)
                nc.scalar.activation(pos[:, t], ps_a[:, t], ACT.Copy).then_inc(pos_copied, 1)

            for i in range(QS):
                act.wait_ge(q_stored[i], 16 * len(range(i, A, QS)))
            act.wait_ge(q_stats_done, A)
            copy_pos(0)
            act.wait_ge(e_loaded[1], 32)
            split_hi(2, 0, 0, 1)
            copy_pos(1)
            split_hi(3, 1, 1, 1)
            for j in range(J):
                kj = keys[:, j].rearrange("p g a k -> p (g a k)")
                act.wait_ge(keys_shifted, j + 1)
                nc.scalar.activation(kj, kj, ACT.Exp).then_inc(keys_exp, 1)
            act.wait_ge(q_var_ready, 1)
            nc.scalar.activation(q_tmp[:, 1:2], q_tmp[:, 0:1], ACT.Sqrt, bias=eps_t[:]).then_inc(q_std_ready, 1)

            def norm_q(t, slot, off):
                nc.scalar.activation(qn[:, slot].rearrange("p (g a h) -> p g a h", g=G, a=A),
                                     q_in_blk[:, bass.ds(off, 1), :].rearrange("p o (a g h) -> p (o g) a h", g=G, a=A),
                                     ACT.Identity, bias=q_shift[:], scale=q_scale[:]).then_inc(qn_ready, 1)

            act.wait_ge(q_affine, 1)
            act.wait_ge(q_blk_loaded, 32)
            norm_q(0, 0, 0)
            norm_q(1, 1, 1)
            act.wait_ge(q_diag_ready, 1)
            norm_q(2, 0, 2)
            act.wait_ge(q_diag_ready, 2)
            norm_q(3, 1, 3)

            with act.Fori(1, TILES // 4) as q:
                for i in range(4):
                    t = 4 * q + i
                    if i % 2 == 0:
                        act.wait_ge(e_loaded[i // 2], (q + 1) * 32)
                    act.wait_ge(pos_summed, t - 1)
                    split_hi(t, i % 2, i % 2, i // 2)
                    if i == 0:
                        act.wait_ge(q_blk_loaded, (q // (BT // 4) + 1) * 32)
                    act.wait_ge(q_diag_ready, t - 1)
                    norm_q(t, i % 2, t % (2 * BT))

        @block.vector
        def _(dve):
            steps = [0]

            def link(ins):
                steps[0] += 1
                ins.then_inc(dve_step, 1)
                dve.wait_ge(dve_step, steps[0])

            dve.wait_ge(consts, 6)
            link(nc.vector.tensor_reduce(fold[:], ident[:].rearrange("p (m k) -> p k m", k=KD), AX.X, ALU.add))
            nc.vector.tensor_copy(same_k[:].rearrange("p (m k) -> p m k", k=KD),
                                  fold[:].unsqueeze(1).to_broadcast([P, TN, KD])).then_inc(same_k_ready, 1)

            def gn_moments(grp, par):
                for i in range(GB):
                    s = par * GB + i
                    dve.wait_ge(x_loaded[s], 16 * (grp // 2 + 1))
                    for half in range(2):
                        ins = nc.vector.bn_stats(bn6[:, s, half], x_in[:, s, half * BANK:(half + 1) * BANK])
                    if i == GB - 1:
                        link(ins)
                for i in range(GB):
                    s = par * GB + i
                    ins = nc.vector.bn_aggr(mv[:, par, i], bn6[:, s].rearrange("p a s -> p (a s)"))
                link(ins)
                link(nc.vector.tensor_tensor(gn_sq[:, par], mv[:, par, :, 0], mv[:, par, :, 0], ALU.mult))
                nc.vector.tensor_copy(gn_in[:, par, :, 0], mv[:, par, :, 0])
                nc.vector.tensor_tensor(gn_in[:, par, :, 1], gn_sq[:, par], mv[:, par, :, 1], ALU.add).then_inc(gn_stats, 1)

            def gn_finish(grp, par):
                dve.wait_ge(gn_summed, grp + 1)
                nc.vector.tensor_copy(gn_out[:, par].rearrange("p b s -> p (b s)"), gn_ps).then_inc(gn_read, 1)
                dve.wait_ge(gn_read, grp + 1)
                link(nc.vector.tensor_tensor(gn_sq[:, par], gn_out[:, par, :, 0], gn_out[:, par, :, 0], ALU.mult))
                nc.vector.tensor_tensor(gn_var[:, par], gn_out[:, par, :, 1], gn_sq[:, par], ALU.subtract).then_inc(gn_var_ready, 1)
                dve.wait_ge(gn_std_ready, grp + 1)
                link(nc.vector.reciprocal(gn_rstd[:, par], gn_std[:, par]))
                nc.vector.scalar_tensor_tensor(gn_bias[:, par], gn_out[:, par, :, 0], -1.0, gn_rstd[:, par],
                                               ALU.mult, ALU.mult).then_inc(gn_ready, 1)

            def value_stats(a):
                dve.wait_ge(proj_read, 8 * a + 8)
                for j in range(J):
                    ins = nc.vector.bn_stats(v_stats[:, j, a], v_nat[:, j, :, a, :])
                return ins

            def query_stats(a):
                dve.wait_ge(proj_read, 8 * a + 8)
                for k in range(KD):
                    ins = nc.vector.bn_stats(q_stats[:, k, a], q_nat[:, a % QS, :, k].rearrange("p j g h -> p j (g h)"))
                return ins.then_inc(q_stats_done, 1)

            between = {3: lambda: value_stats(0), 4: lambda: query_stats(0), 5: lambda: value_stats(1),
                       7: lambda: (value_stats(2), query_stats(1), query_stats(2))}
            for grp in range(B // GB):
                gn_moments(grp, grp % 2)
                gn_finish(grp, grp % 2)
                if grp in between:
                    between[grp]()
            link(value_stats(A - 1))

            for j in range(J):
                ins = nc.vector.bn_aggr(v_mv[:, j], v_stats[:, j].rearrange("p a s -> p (a s)"))
            ins.then_inc(v_var_ready, 1)
            dve.wait_ge(v_std_ready, 1)
            dve.wait_ge(params_loaded, 16 * (2 + 2 * TN))
            link(nc.vector.reciprocal(v_tmp[:], v_std[:]))
            link(nc.vector.tensor_tensor(v_scale[:], v_tmp[:], gam_v[:], ALU.mult))
            link(nc.vector.tensor_tensor(v_tmp[:], v_mv[:, :, 0], v_scale[:], ALU.mult))
            nc.vector.tensor_tensor(v_shift[:], bet_v[:], v_tmp[:], ALU.subtract).then_inc(v_affine, 1)

            def split_lo(slot, off, k, t):
                dve.wait_ge(e_hi_ready, t + 1)
                nc.vector.tensor_tensor(e_lo[:, slot],
                                        e_nat[:, k, off * TN:(off + 1) * TN, :].rearrange("p n (j k) -> p j n k", j=J),
                                        e_hi[:, slot].bitcast(f32), ALU.subtract).then_inc(e_lo_ready, 1)

            split_lo(0, 0, 0, 0)
            for j in range(J):
                dve.wait_ge(v_hi_ready, j + 1)
                nc.vector.tensor_tensor(v_lo[:, j], v_nat[:, j].rearrange("p g a v -> p (g a v)"),
                                        v_hi[:, j].bitcast(f32), ALU.subtract).then_inc(v_lo_ready, 1)
            split_lo(1, 1, 0, 1)
            nc.vector.tensor_reduce(key_max[:], keys[:].rearrange("p j g a k -> p (g a k) j"), AX.X,
                                    ALU.max).then_inc(key_max_ready, 1)
            query_stats(A - 1)
            split_lo(0, 0, 1, 2)
            dve.wait_ge(key_top_ready, 1)
            for j in range(J):
                kj = keys[:, j].rearrange("p g a k -> p (g a k)")
                nc.vector.tensor_tensor(kj, kj, key_top[:], ALU.subtract).then_inc(keys_shifted, 1)

            dve.wait_ge(q_stats_done, A)
            for k in range(KD):
                ins = nc.vector.bn_aggr(q_mv[:, k], q_stats[:, k].rearrange("p a s -> p (a s)"))
            link(ins)
            link(nc.vector.tensor_tensor(q_sq[:], q_mv[:, :, 0], q_mv[:, :, 0], ALU.mult))
            link(nc.vector.tensor_tensor(q_sq[:], q_sq[:], q_mv[:, :, 1], ALU.add))
            nc.vector.tensor_copy(q_in[:, 0], q_mv[:, :, 0].unsqueeze(1).to_broadcast([P, TN, KD]))
            nc.vector.tensor_copy(q_in[:, 1], q_sq[:].unsqueeze(1).to_broadcast([P, TN, KD])).then_inc(q_moments, 1)
            split_lo(1, 1, 1, 3)
            dve.wait_ge(q_averaged, 1)
            link(nc.vector.tensor_copy(q_out[:], q_ps))
            link(nc.vector.tensor_tensor(q_tmp[:, 2:3], q_out[:, 0:1], q_out[:, 0:1], ALU.mult))
            nc.vector.tensor_tensor(q_tmp[:, 0:1], q_out[:, 1:2], q_tmp[:, 2:3], ALU.subtract).then_inc(q_var_ready, 1)
            dve.wait_ge(q_std_ready, 1)
            link(nc.vector.reciprocal(q_tmp[:, 2:3], q_tmp[:, 1:2]))
            link(nc.vector.tensor_tensor(q_scale[:], q_tmp[:, 2:3], gam_q[:], ALU.mult))
            link(nc.vector.tensor_tensor(q_tmp[:, 3:4], q_out[:, 0:1], q_scale[:], ALU.mult))
            nc.vector.tensor_tensor(q_shift[:], bet_q[:], q_tmp[:, 3:4], ALU.subtract).then_inc(q_affine, 1)
            for i in range(QS):
                dve.wait_ge(q_stored[i], 16 * len(range(i, A, QS)))
            dve.wait_ge(lam_summed, 1)
            link(nc.vector.reciprocal(inv_sum[:], ps_b[:, 1, 0:B // TN]))
            dve.wait_ge(lam_zeroed, 1)
            for g in range(G):
                s, half = g // 2, g % 2
                rows = slice(half * HALF, (half + 1) * HALF)
                nc.vector.scalar_tensor_tensor(
                    lam_diag[rows, g * P:(g + 1) * P].rearrange("p (a v) -> p a v", v=V),
                    ps_b[rows, 0, s * P:(s + 1) * P].rearrange("p (a v) -> p a v", v=V),
                    inv_sum[rows, s:s + 1], row_mask[rows, half * A:(half + 1) * A].unsqueeze(2).to_broadcast([HALF, A, V]),
                    ALU.mult, ALU.mult).then_inc(lam_masked, 1)
            dve.wait_ge(lam_spread, 1)
            link(nc.vector.tensor_copy(content[:], ps_b[:, 1]))

            def read_pos(t, slot):
                dve.wait_ge(pos_summed, t + 1)
                nc.vector.tensor_tensor(pos[:, slot], ps_a[:, slot], content[:], ALU.add).then_inc(pos_ready, 1)

            def add_out(t, slot, off):
                dve.wait_ge(queried, t + 1)
                for a in range(A):
                    rows = slice(a * V, (a + 1) * V)
                    r = res[rows, :, bass.ds(off, TN)].rearrange("v (g h) n -> v g h n", h=NH)
                    ins = nc.vector.tensor_tensor(
                        r, ps_b[rows, slot, 0:G * HALF].rearrange("v (g a h n) -> v g a h n", g=G, a=2, h=NH)[:, :, a % 2],
                        r, ALU.add)
                ins.then_inc(res_added, 1)

            for t in range(2):
                dve.wait_ge(pos_copied, t + 1)
                nc.vector.tensor_tensor(pos[:, t], pos[:, t], content[:], ALU.add).then_inc(pos_ready, 1)
            dve.wait_ge(res_loaded, 16 * A)
            add_out(0, 0, 0)

            with dve.Fori(0, TILES // 4 - 1) as q:
                for i in range(4):
                    t = 4 * q + 2 + i
                    read_pos(t, i % 2)
                    split_lo(i % 2, i % 2, i // 2, t + 2)
                    if i == 3:
                        dve.wait_ge(res_loaded, ((q + 1) // (BT // 4) + 1) * (16 * A))
                    add_out(t - 1, (i + 1) % 2, ((t - 1) % (2 * BT)) * TN)
            read_pos(TILES - 2, 0)
            add_out(TILES - 3, 1, 2 * BN - 3 * TN)
            read_pos(TILES - 1, 1)
            add_out(TILES - 2, 0, 2 * BN - 2 * TN)
            add_out(TILES - 1, 1, 2 * BN - TN)

        @block.tensor
        def _(pe):
            pe.wait_ge(consts, 4)
            pe.wait_ge(weights_loaded, 16 * 3)
            nc.tensor.transpose(ps_a[:, 0, 0:PC], w_rows[:], ident[0:PC, 0:PC]).then_inc(w_transposed, 1)
            pe.wait_ge(consts, 6)

            def gn_average(grp, par, reads):
                pe.wait_ge(gn_stats, grp + 1)
                if reads:
                    pe.wait_ge(proj_read, reads)
                nc.tensor.matmul(gn_ps, group_avg[:], gn_in[:, par].rearrange("p b s -> p (b s)"),
                                 start=True, stop=True).then_inc(gn_summed, 1)

            def transpose_image(b, i):
                pe.wait_ge(x_normed, b + 1)
                if b >= 2:
                    pe.wait_ge(xt_ready, b - 1)
                for j in range(J):
                    ins = nc.tensor.transpose(ps_a[:, i % 2, j * C:(j + 1) * C], x_in[:, i, j * D:(j + 1) * D], ident[:])
                ins.then_inc(x_transposed, 1)

            def project(b, i):
                pe.wait_ge(xt_ready, b + 1)
                if i % GB == 2:
                    pe.wait_ge(gn_read, min(b // GB + 2, B // GB))
                if b >= 2:
                    pe.wait_ge(proj_read, b - 1)
                for j in range(J):
                    ins = nc.tensor.matmul(ps_b[:, i % 2, j * P:j * P + PC], x_t[:, i % 2, j * C:(j + 1) * C], w_cols[:],
                                           start=True, stop=True)
                ins.then_inc(projected, 1)

            gn_average(0, 0, 0)
            pe.wait_ge(gn_read, 1)
            pe.wait_ge(w_ready, 1)
            for a in range(A):
                for i in range(G):
                    b = 8 * a + i
                    transpose_image(b, i)
                    if b > 0:
                        project(b - 1, (i - 1) % G)
                    if i == 2:
                        gn_average(2 * a + 1, 1, b - 1)
                    if i == 6 and a < A - 1:
                        gn_average(2 * a + 2, 0, b - 1)
            project(B - 1, G - 1)

            def sum_tile(t, slot, first=False, half_way=None):
                pe.wait_ge(e_hi_ready, t + 1)
                pe.wait_ge(e_lo_ready, t + 1)
                for j in range(J):
                    if first:
                        pe.wait_ge(v_lo_ready, j + 1)
                    if half_way and j == J // 2:
                        half_way()
                    for n, (e, v) in enumerate(((e_hi, v_hi), (e_hi, v_lo), (e_lo, v_hi))):
                        for half in range(BV // BANK):
                            cols = slice(half * BANK, (half + 1) * BANK)
                            ins = nc.tensor.matmul(ps_a[:, slot, cols], e[:, slot, j].rearrange("p n k -> p (n k)"),
                                                   v[:, j, cols], start=(j == 0 and n == 0), stop=(j == J - 1 and n == 2))
                ins.then_inc(pos_summed, 1)

            def query_tile(t, slot):
                pe.wait_ge(pos_ready, t + 1)
                pe.wait_ge(q_diag_ready, t + 1)
                for g in range(G):
                    for half in range(2):
                        cols = slice(g * P + half * HALF, g * P + (half + 1) * HALF)
                        ins = nc.tensor.matmul(ps_b[half * HALF:(half + 1) * HALF, slot, g * HALF:(g + 1) * HALF],
                                               pos[:, slot, cols], q_diag[:, slot, cols], start=True, stop=True)
                ins.then_inc(queried, 1)

            pe.wait_ge(proj_read, B)
            sum_tile(0, 0, first=True)
            sum_tile(1, 1)
            pe.wait_ge(pos_copied, 1)
            sum_tile(2, 0)
            pe.wait_ge(q_moments, 1)
            for s in range(2):
                ins = nc.tensor.matmul(q_ps[:, s:s + 1], q_in[:, s].rearrange("p n k -> p (n k)"), inv_p[:],
                                       start=True, stop=True)
            ins.then_inc(q_averaged, 1)
            pe.wait_ge(keys_exp, J)
            for s in range(B // TN):
                for j in range(J):
                    for half in range(2):
                        nc.tensor.matmul(ps_b[half * HALF:(half + 1) * HALF, 0, s * P:(s + 1) * P],
                                         keys[:, j, 2 * s + half].rearrange("p a k -> p (a k)"),
                                         v_nat[:, j, 2 * s + half].rearrange("p a v -> p (a v)"),
                                         start=(j == 0), stop=(j == J - 1))
            pe.wait_ge(exp_summed, 1)
            for s in range(B // TN):
                ins = nc.tensor.matmul(ps_b[:, 1, s:s + 1], exp_sum[:, s * P:(s + 1) * P], ones[:], start=True, stop=True)
            ins.then_inc(lam_summed, 1)

            def spread_content():
                pe.wait_ge(same_k_ready, 1)
                pe.wait_ge(q_var_ready, 1)
                pe.wait_ge(lam_masked, G)
                for s in range(B // TN):
                    cols = slice(s * TN * V, (s + 1) * TN * V)
                    ins = nc.tensor.matmul(ps_b[:, 1, cols], same_k[:], lam_diag[:, cols], start=True, stop=True)
                ins.then_inc(lam_spread, 1)

            pe.wait_ge(pos_copied, 2)
            sum_tile(3, 1, half_way=spread_content)
            query_tile(0, 0)
            query_tile(1, 1)
            query_tile(2, 0)
            with pe.Fori(1, TILES // 4) as q:
                for i in range(4):
                    sum_tile(4 * q + i, i % 2)
                    query_tile(4 * q + i - 1, (i + 1) % 2)
            query_tile(TILES - 1, 1)


_INS = ["x", "L0_conv_Wq", "L0_conv_Wk", "L0_conv_Wv", "L0_conv_E", "L0_conv_gamma_v", "L0_conv_beta_v",
        "L0_conv_gamma_q", "L0_conv_beta_q"]


def kernel(**inputs):
    import numpy as _np
    import concourse.bacc as _bacc
    from concourse import mybir as _mybir
    from concourse.bass_utils import run_bass_kernel_spmd as _run

    nc = _bacc.Bacc("TRN2", target_bir_lowering=False, num_devices=1)
    arrays, args = {}, []
    for name in _INS:
        a = _np.ascontiguousarray(inputs[name])
        arrays[f"in_{name}"] = a
        args.append(nc.dram_tensor(f"in_{name}", a.shape, _mybir.dt.from_np(a.dtype), kind="ExternalInput").ap())
    shape = arrays["in_x"].shape
    args.append(nc.dram_tensor("out_dram", shape, _mybir.dt.float32, kind="ExternalOutput").ap())
    lambda_conv_kernel(nc, *args)
    r = _run(nc, [arrays], core_ids=[0])
    return r.results[0]["out_dram"]
```

```python
import concourse.bass as bass
from concourse import mybir
from contextlib import ExitStack


def lambda_conv_kernel(nc: bass.Bass, x, Wq, Wk, Wv, E, gamma_v, beta_v, gamma_q, beta_q, out):
    f32 = mybir.dt.float32
    f32r = mybir.dt.float32r
    ALU = mybir.AluOpType
    ACT = mybir.ActivationFunctionType
    AX = mybir.AxisListType
    RMAX = bass.bass_isa.ReduceOp.max

    P = 128
    B, C, H, W = x.shape
    D = C
    J = H * W // D
    N = H * W
    KD = Wk.shape[0]
    NH = Wq.shape[0] // KD
    V = Wv.shape[0]
    A = P // V
    G = B // A
    BV = B * V
    BH = B * NH
    QC, KC = KD * NH, KD
    PC = QC + KC + V
    TN = P // KD
    TILES = N // TN
    HALF = P // 2
    BANK = 512
    BT = 16
    BLOCKS = TILES // BT
    BN = BT * TN
    PAIRS = TILES // 2
    PPB = BT // 2
    GB = 4
    SLOTS = 2 * GB
    BATCHES = [(0, GB // 2), (GB // 2, GB // 2)] + [(b, GB) for b in range(GB, B, GB)]
    QS = 3
    GN_C = C // 32
    EPS = 1e-5

    ctx = ExitStack()

    def sb(name, shape, dt=f32, stack=ctx):
        return stack.enter_context(nc.sbuf_tensor(name, shape, dt))

    with ctx:
        ident = sb("ident", [P, P])
        group_avg = sb("group_avg", [P, P])
        same_k = sb("same_k", [P, P])
        row_mask = sb("row_mask", [P, TN])
        fold = sb("fold", [P, KD])
        ones = sb("ones", [P, 1])
        inv_p = sb("inv_p", [P, 1])
        eps_t = sb("eps_t", [P, 1])
        sqrt_first = sb("sqrt_first", [P, 1])
        w_rows = sb("w_rows", [PC, D])
        w_cols = sb("w_cols", [D, PC])
        gam_v = sb("gam_v", [P, J])
        bet_v = sb("bet_v", [P, J])
        gam_q = sb("gam_q", [P, 1])
        bet_q = sb("bet_q", [P, 1])
        bn6 = sb("bn6", [P, SLOTS, 2, 6])
        mv = sb("mv", [P, SLOTS, 2])
        gn_in = sb("gn_in", [P, SLOTS, 2])
        gn_sq = sb("gn_sq", [P, SLOTS])
        gn_out = sb("gn_out", [P, SLOTS, 2])
        gn_var = sb("gn_var", [P, SLOTS])
        gn_std = sb("gn_std", [P, SLOTS])
        gn_rstd = sb("gn_rstd", [P, SLOTS])
        gn_bias = sb("gn_bias", [P, SLOTS])
        v_stats = sb("v_stats", [P, J, A, 6])
        q_stats = sb("q_stats", [P, KD, A, 6])
        v_mv = sb("v_mv", [P, J, 2])
        v_std = sb("v_std", [P, J])
        v_scale = sb("v_scale", [P, J])
        v_tmp = sb("v_tmp", [P, J])
        v_shift = sb("v_shift", [P, J])
        q_mv = sb("q_mv", [P, KD, 2])
        q_in = sb("q_in", [P, 2, TN, KD])
        q_sq = sb("q_sq", [P, KD])
        q_out = sb("q_out", [P, 2])
        q_tmp = sb("q_tmp", [P, 4])
        q_scale = sb("q_scale", [P, 1])
        q_shift = sb("q_shift", [P, 1])
        key_max = sb("key_max", [P, B * KD])
        key_top = sb("key_top", [P, B * KD])
        exp_sum = sb("exp_sum", [P, B * KD])
        inv_sum = sb("inv_sum", [P, B // TN])
        qn = sb("qn", [P, 2, BH])
        e_nat = sb("e_nat", [P, 2, 2 * TN, J * KD])
        e_hi = sb("e_hi", [P, 2, J, TN, KD], f32r)
        e_lo = sb("e_lo", [P, 2, J, TN, KD], f32r)

        keys = sb("keys", [P, J, G, A, KD])
        early = ExitStack()
        x_in = sb("x_in", [P, SLOTS, J * D], stack=early)
        x_t = sb("x_t", [D, 2, J * C], stack=early)
        early.close()
        v_hi = sb("v_hi", [P, J, BV], f32r)
        v_lo = sb("v_lo", [P, J, BV], f32r)
        early = ExitStack()
        q_nat = sb("q_nat", [P, QS, J, KD, G, NH], stack=early)
        v_nat = sb("v_nat", [P, J, G, A, V], stack=early)
        early.close()
        q_in_blk = sb("q_in_blk", [P, 2 * BT, BH])
        pos = sb("pos", [P, 2, BV])
        q_diag = sb("q_diag", [P, 2, B * NH * TN])
        lam_diag = sb("lam_diag", [P, BV])
        content = sb("content", [P, BV])
        res = sb("res", [P, G * NH, 2 * BN])

        ps_a = ctx.enter_context(nc.psum_tensor("ps_a", [P, 2, BV], f32))
        ps_b = ctx.enter_context(nc.psum_tensor("ps_b", [P, 2, BV], f32))
        q_dram = nc.dram_tensor("q_dram", (C, A, J * KD, G * NH), f32).ap()
        q_ps = ps_b[:, 1, BANK:BANK + 2]
        gn_ps = ps_b[:, 0, 0:2 * GB]

        def slots(k):
            b, count = BATCHES[k]
            return slice(b % SLOTS, b % SLOTS + count)

        def sem(name):
            return ctx.enter_context(nc.semaphore(name))

        x_loaded = [sem(f"x_loaded{i}") for i in range(SLOTS)]
        weights_loaded = sem("weights_loaded")
        params_loaded = sem("params_loaded")
        memsets = sem("memsets")
        consts = sem("consts")
        w_transposed = sem("w_transposed")
        w_ready = sem("w_ready")
        same_k_ready = sem("same_k_ready")
        gn_stats = sem("gn_stats")
        gn_summed = sem("gn_summed")
        gn_read = sem("gn_read")
        gn_var_ready = sem("gn_var_ready")
        gn_std_ready = sem("gn_std_ready")
        gn_ready = sem("gn_ready")
        x_normed = sem("x_normed")
        x_transposed = sem("x_transposed")
        xt_ready = sem("xt_ready")
        projected = sem("projected")
        values_read = sem("values_read")
        proj_read = sem("proj_read")
        q_stats_done = sem("q_stats_done")
        q_stored = [sem(f"q_stored{i}") for i in range(QS)]
        dve_step = sem("dve_step")
        v_var_ready = sem("v_var_ready")
        v_std_ready = sem("v_std_ready")
        v_affine = sem("v_affine")
        v_normed = sem("v_normed")
        v_hi_ready = sem("v_hi_ready")
        v_lo_ready = sem("v_lo_ready")
        key_max_ready = sem("key_max_ready")
        key_top_ready = sem("key_top_ready")
        keys_shifted = sem("keys_shifted")
        keys_exp = sem("keys_exp")
        exp_summed = sem("exp_summed")
        q_moments = sem("q_moments")
        q_averaged = sem("q_averaged")
        q_var_ready = sem("q_var_ready")
        q_std_ready = sem("q_std_ready")
        q_affine = sem("q_affine")
        lam_summed = sem("lam_summed")
        lam_zeroed = sem("lam_zeroed")
        lam_masked = sem("lam_masked")
        lam_spread = sem("lam_spread")
        e_loaded = [sem(f"e_loaded{i}") for i in range(2)]
        e_hi_ready = sem("e_hi_ready")
        e_lo_ready = sem("e_lo_ready")
        pos_summed = sem("pos_summed")
        pos_copied = sem("pos_copied")
        pos_ready = sem("pos_ready")
        pool_step = sem("pool_step")
        q_blk_loaded = sem("q_blk_loaded")
        qn_ready = sem("qn_ready")
        q_diag_ready = sem("q_diag_ready")
        queried = sem("queried")
        res_loaded = sem("res_loaded")
        res_added = sem("res_added")
        res_stored = sem("res_stored")

        x_v = x.rearrange("b c y z -> c b (y z)")
        e_v = E.rearrange("n (p j) k -> p n (j k)", j=J)
        x_q = x.rearrange("b (h v) y z -> v (b h) (y z)", v=V)
        out_q = out.rearrange("b (h v) y z -> v (b h) (y z)", v=V)
        q_dram_v = q_dram.rearrange("c a p f -> p (c a) f")

        block = ctx.enter_context(nc.Block())

        @block.sync
        def _(sp):
            def load_x(b, i):
                sp.dma_start(x_in[:, i, :], x_v[:, bass.ds(b, 1), :]).then_inc(x_loaded[i], 16)

            def held(value):
                return value if isinstance(value, int) else sp.snap(value)

            def load_e(n, slot):
                for h in range(2):
                    sp.dma_start(e_nat[:, slot, h * TN:(h + 1) * TN],
                                 e_v[:, bass.ds(n[h], TN), :]).then_inc(e_loaded[slot], 16)

            def load_q(at, to):
                for h in range(2):
                    rows = BT // 2
                    sp.dma_start(q_in_blk[:, bass.ds(to + h * rows, rows), :].rearrange("p c (a f) -> p (c a) f", a=A),
                                 q_dram_v[:, bass.ds((at + h * rows) * A, rows * A), :]).then_inc(q_blk_loaded, 16)

            def load_res(at, col):
                for a in range(A):
                    sp.dma_start(res[a * V:(a + 1) * V, :, bass.ds(col, BN)],
                                 x_q[:, a * G * NH:(a + 1) * G * NH, bass.ds(at, BN)]).then_inc(res_loaded, 16)

            def store_res(at, col, quadrants=range(A)):
                for a in quadrants:
                    sp.dma_start(out_q[:, a * G * NH:(a + 1) * G * NH, bass.ds(at, BN)],
                                 res[a * V:(a + 1) * V, :, bass.ds(col, BN)]).then_inc(res_stored, 16)

            def store_q(a):
                sp.wait_ge(proj_read, 8 * a + 8)
                sp.dma_start(q_dram[:, a], q_nat[:, a % QS].rearrange("p j k g h -> p (j k) (g h)")
                             ).then_inc(q_stored[a % QS], 16)

            for i in range(GB // 2):
                load_x(i, i)
            sp.dma_start(w_rows[0:QC, :], Wq).then_inc(weights_loaded, 16)
            sp.dma_start(w_rows[QC:QC + KC, :], Wk).then_inc(weights_loaded, 16)
            sp.dma_start(w_rows[QC + KC:PC, :], Wv).then_inc(weights_loaded, 16)
            for i in range(GB // 2, SLOTS):
                load_x(i, i)
            sp.dma_start(gam_v[:, :], gamma_v.rearrange("(p j) -> p j", j=J)).then_inc(params_loaded, 16)
            sp.dma_start(bet_v[:, :], beta_v.rearrange("(p j) -> p j", j=J)).then_inc(params_loaded, 16)
            for n in range(TN):
                sp.dma_start(gam_q[n * KD:(n + 1) * KD, :], gamma_q.rearrange("(k a) -> k a", a=1)).then_inc(params_loaded, 16)
                sp.dma_start(bet_q[n * KD:(n + 1) * KD, :], beta_q.rearrange("(k a) -> k a", a=1)).then_inc(params_loaded, 16)
            for a in range(A - 1):
                for i in range(G):
                    sp.wait_ge(x_transposed, 8 * a + i + 1)
                    load_x(8 * (a + 1) + i, i)
                    if a > 0 and i == 2:
                        store_q(a - 1)
            load_e((0, TN), 0)
            load_e((2 * TN, 3 * TN), 1)
            store_q(A - 2)
            store_q(A - 1)
            for i in range(QS):
                sp.wait_ge(q_stored[i], 16 * len(range(i, A, QS)))
            sp.wait_ge(q_stats_done, A)
            load_q(0, 0)
            sp.wait_ge(lam_summed, 1)
            load_res(0, 0)

            def e_pair(p, slot):
                n = held(p * 2 * TN), held(p * 2 * TN + TN)
                sp.wait_ge(e_lo_ready, 2 * p - 2)
                load_e(n, slot)

            def loads_of_block(blk):
                first, last = isinstance(blk, int) and blk == 0, isinstance(blk, int) and blk == BLOCKS - 1
                if not first:
                    before, col = held((blk - 1) * BN), held(((blk + 1) % 2) * BN)
                if not last:
                    after, to = held((blk + 1) * BN), held(((blk + 1) % 2) * BN)
                    q_at, q_to = held((blk + 1) * BT), held(((blk + 1) % 2) * BT)
                for p in range(2, PPB + 2):
                    if last and last_pair(p):
                        return
                    e_pair(blk * PPB + p, p % 2)
                    if p == 3 and not first:
                        sp.wait_ge(res_added, blk * BT)
                        store_res(before, col)
                    if p == PPB and not last:
                        sp.wait_ge(qn_ready, blk * BT + (BT - 3))
                        load_q(q_at, q_to)
                if not first:
                    sp.wait_ge(res_stored, blk * (16 * A))
                sp.wait_ge(res_added, blk * BT + (BT - 3))
                load_res(after, to)

            def last_pair(p):
                return (BLOCKS - 1) * PPB + p >= PAIRS

            loads_of_block(0)
            with sp.Fori(1, BLOCKS - 1) as blk:
                loads_of_block(blk)
            loads_of_block(BLOCKS - 1)
            last = BLOCKS - 1
            for a in range(A):
                sp.wait_ge(res_added, TILES - 1 + a + 1)
                store_res(last * BN, last % 2 * BN, quadrants=[a])
            sp.wait_ge(res_stored, BLOCKS * 16 * A)

        @block.gpsimd
        def _(pool):
            pool.memset(ident[:], 0.0).then_inc(memsets, 1)
            pool.memset(group_avg[:], 1.0 / GN_C).then_inc(memsets, 1)
            pool.memset(row_mask[:], 1.0).then_inc(memsets, 1)
            pool.memset(ones[:], 1.0).then_inc(consts, 1)
            pool.memset(inv_p[:], 1.0 / P).then_inc(consts, 1)
            pool.memset(eps_t[:], EPS).then_inc(consts, 1)
            pool.wait_ge(memsets, 3)
            pool.affine_select(out=ident[:], in_=ident[:], compare_op=ALU.not_equal, fill=1.0, base=0,
                               pattern=[[-1, P]], channel_multiplier=1).then_inc(consts, 1)
            avg_v = group_avg[:].rearrange("p (g i) -> p g i", i=GN_C)
            pool.affine_select(out=avg_v, in_=avg_v, compare_op=ALU.is_ge, fill=0.0, base=0,
                               pattern=[[-GN_C, C // GN_C], [0, GN_C]], channel_multiplier=1).then_inc(memsets, 1)
            pool.affine_select(out=row_mask[:], in_=row_mask[:], compare_op=ALU.is_ge, fill=0.0, base=0,
                               pattern=[[-KD, TN]], channel_multiplier=1).then_inc(memsets, 1)
            pool.wait_ge(memsets, 5)
            pool.affine_select(out=avg_v, in_=avg_v, compare_op=ALU.is_ge, fill=0.0, base=GN_C - 1,
                               pattern=[[GN_C, C // GN_C], [0, GN_C]], channel_multiplier=-1).then_inc(consts, 1)
            pool.affine_select(out=row_mask[:], in_=row_mask[:], compare_op=ALU.is_ge, fill=0.0, base=KD - 1,
                               pattern=[[KD, TN]], channel_multiplier=-1).then_inc(consts, 1)

            def norm_images(k):
                pool.wait_ge(gn_ready, k + 1)
                for i in range(slots(k).start, slots(k).stop):
                    xi = x_in[:, i, :]
                    pool.tensor_scalar(xi, xi, gn_rstd[:, i:i + 1], gn_bias[:, i:i + 1],
                                       ALU.mult, ALU.add).then_inc(x_normed, 1)

            for k in range(len(BATCHES)):
                norm_images(k)

            pool.wait_ge(v_affine, 1)
            for j in range(J):
                vj = v_nat[:, j].rearrange("p g a v -> p (g a v)")
                pool.tensor_scalar(vj, vj, v_scale[:, j:j + 1], v_shift[:, j:j + 1],
                                   ALU.mult, ALU.add).then_inc(v_normed, 1)
            pool.wait_ge(key_max_ready, 1)
            pool.partition_all_reduce(key_top[:], key_max[:], P, RMAX).then_inc(key_top_ready, 1)
            for j in range(1, J):
                kj = keys[:, j].rearrange("p g a k -> p (g a k)")
                before = keys[:, 0].rearrange("p g a k -> p (g a k)") if j == 1 else exp_sum[:]
                pool.wait_ge(keys_exp, j + 1)
                if j > 1:
                    pool.wait_ge(pool_step, j - 1)
                pool.tensor_tensor(exp_sum[:], before, kj, ALU.add).then_inc(pool_step if j < J - 1 else exp_summed, 1)

            def diag(t, slot):
                pool.wait_ge(qn_ready, t + 1)
                pool.tensor_tensor(q_diag[:, slot].rearrange("p (q n) -> p q n", n=TN),
                                   qn[:, slot].unsqueeze(2).to_broadcast([P, BH, TN]),
                                   row_mask[:].unsqueeze(1).to_broadcast([P, BH, TN]),
                                   ALU.mult).then_inc(q_diag_ready, 1)

            for i in range(QS):
                pool.wait_ge(q_stored[i], 16 * len(range(i, A, QS)))
            pool.wait_ge(q_stats_done, A)
            pool.memset(lam_diag[:], 0.0).then_inc(lam_zeroed, 1)
            diag(0, 0)
            diag(1, 1)
            with pool.Fori(1, TILES // 2) as p:
                for i in range(2):
                    pool.wait_ge(queried, 2 * p + i - 1)
                    diag(2 * p + i, i)

        @block.scalar
        def _(act):
            act.wait_ge(consts, 3)
            nc.scalar.activation(sqrt_first[:], eps_t[:], ACT.Sqrt)
            act.wait_ge(w_transposed, 1)
            nc.scalar.activation(w_cols[:], ps_a[:, 0, 0:PC], ACT.Copy).then_inc(w_ready, 1)

            def gn_sqrt(k):
                act.wait_ge(gn_var_ready, k + 1)
                nc.scalar.activation(gn_std[:, slots(k)], gn_var[:, slots(k)], ACT.Sqrt, bias=eps_t[:]).then_inc(gn_std_ready, 1)

            def read_xt(b, i, first):
                act.wait_ge(x_transposed, b + 1)
                if not (first and i < 2):
                    act.wait_ge(projected, b - 1)
                nc.scalar.activation(x_t[:, i % 2], ps_a[:, i % 2], ACT.Copy).then_inc(xt_ready, 1)

            def read_proj(b, a, i, slot):
                act.wait_ge(projected, b + 1)
                pr = ps_b[:, i % 2].rearrange("p (j f) -> p j f", f=P)
                nc.scalar.activation(v_nat[:, :, i, bass.ds(a, 1), :].rearrange("p j a v -> p j (a v)"),
                                     pr[:, :, QC + KC:PC], ACT.Copy).then_inc(values_read, 1)
                nc.scalar.activation(keys[:, :, i, bass.ds(a, 1), :].rearrange("p j a v -> p j (a v)"),
                                     pr[:, :, QC:QC + KC], ACT.Copy)
                nc.scalar.activation(q_nat[:, slot, :, :, i, :],
                                     pr[:, :, 0:QC].rearrange("p j (k h) -> p j k h", h=NH),
                                     ACT.Copy).then_inc(proj_read, 1)

            gn_sqrt(0)
            for a in range(A):
                if a >= QS:
                    act.wait_ge(q_stored[a % QS], 16 * (a // QS))
                    act.wait_ge(q_stats_done, a - QS + 1)
                for i in range(G):
                    read_xt(8 * a + i, i, a == 0)
                    if i > 0:
                        read_proj(8 * a + i - 1, a, i - 1, a % QS)
                    if a == 0 and i == 0:
                        gn_sqrt(1)
                    if i == 2:
                        gn_sqrt(2 * a + 2)
                    if i == 6 and a < A - 1:
                        gn_sqrt(2 * a + 3)
                read_proj(8 * a + G - 1, a, G - 1, a % QS)

            def split_hi(t, slot, off, k):
                nc.scalar.activation(e_hi[:, slot],
                                     e_nat[:, k, off * TN:(off + 1) * TN, :].rearrange("p n (j k) -> p j n k", j=J),
                                     ACT.Copy).then_inc(e_hi_ready, 1)

            act.wait_ge(e_loaded[0], 32)
            split_hi(0, 0, 0, 0)
            split_hi(1, 1, 1, 0)
            act.wait_ge(v_var_ready, 1)
            nc.scalar.activation(v_std[:], v_mv[:, :, 1], ACT.Sqrt, bias=eps_t[:]).then_inc(v_std_ready, 1)
            for j in range(J):
                act.wait_ge(v_normed, j + 1)
                nc.scalar.activation(v_hi[:, j], v_nat[:, j].rearrange("p g a v -> p (g a v)"),
                                     ACT.Copy).then_inc(v_hi_ready, 1)

            def copy_pos(t):
                act.wait_ge(pos_summed, t + 1)
                nc.scalar.activation(pos[:, t], ps_a[:, t], ACT.Copy).then_inc(pos_copied, 1)

            for i in range(QS):
                act.wait_ge(q_stored[i], 16 * len(range(i, A, QS)))
            act.wait_ge(q_stats_done, A)
            copy_pos(0)
            act.wait_ge(e_loaded[1], 32)
            split_hi(2, 0, 0, 1)
            copy_pos(1)
            split_hi(3, 1, 1, 1)
            for j in range(J):
                kj = keys[:, j].rearrange("p g a k -> p (g a k)")
                act.wait_ge(keys_shifted, j + 1)
                nc.scalar.activation(kj, kj, ACT.Exp).then_inc(keys_exp, 1)
            act.wait_ge(q_var_ready, 1)
            nc.scalar.activation(q_tmp[:, 1:2], q_tmp[:, 0:1], ACT.Sqrt, bias=eps_t[:]).then_inc(q_std_ready, 1)

            def norm_q(t, slot, off):
                nc.scalar.activation(qn[:, slot].rearrange("p (g a h) -> p g a h", g=G, a=A),
                                     q_in_blk[:, bass.ds(off, 1), :].rearrange("p o (a g h) -> p (o g) a h", g=G, a=A),
                                     ACT.Identity, bias=q_shift[:], scale=q_scale[:]).then_inc(qn_ready, 1)

            act.wait_ge(q_affine, 1)
            act.wait_ge(q_blk_loaded, 32)
            norm_q(0, 0, 0)
            norm_q(1, 1, 1)
            act.wait_ge(q_diag_ready, 1)
            norm_q(2, 0, 2)
            act.wait_ge(q_diag_ready, 2)
            norm_q(3, 1, 3)

            with act.Fori(1, TILES // 4) as q:
                for i in range(4):
                    t = 4 * q + i
                    if i % 2 == 0:
                        act.wait_ge(e_loaded[i // 2], (q + 1) * 32)
                    act.wait_ge(pos_summed, t - 1)
                    split_hi(t, i % 2, i % 2, i // 2)
                    if i == 0:
                        act.wait_ge(q_blk_loaded, (q // (BT // 4) + 1) * 32)
                    act.wait_ge(q_diag_ready, t - 1)
                    norm_q(t, i % 2, t % (2 * BT))

        @block.vector
        def _(dve):
            steps = [0]

            def link(ins):
                steps[0] += 1
                ins.then_inc(dve_step, 1)
                dve.wait_ge(dve_step, steps[0])

            dve.wait_ge(consts, 6)
            link(nc.vector.tensor_reduce(fold[:], ident[:].rearrange("p (m k) -> p k m", k=KD), AX.X, ALU.add))
            nc.vector.tensor_copy(same_k[:].rearrange("p (m k) -> p m k", k=KD),
                                  fold[:].unsqueeze(1).to_broadcast([P, TN, KD])).then_inc(same_k_ready, 1)

            def gn_moments(k):
                sl = slots(k)
                for s in range(sl.start, sl.stop):
                    dve.wait_ge(x_loaded[s], 16 * (BATCHES[k][0] // SLOTS + 1))
                    for half in range(2):
                        ins = nc.vector.bn_stats(bn6[:, s, half], x_in[:, s, half * BANK:(half + 1) * BANK])
                link(ins)
                for s in range(sl.start, sl.stop):
                    ins = nc.vector.bn_aggr(mv[:, s], bn6[:, s].rearrange("p a s -> p (a s)"))
                link(ins)
                link(nc.vector.tensor_tensor(gn_sq[:, sl], mv[:, sl, 0], mv[:, sl, 0], ALU.mult))
                nc.vector.tensor_copy(gn_in[:, sl, 0], mv[:, sl, 0])
                nc.vector.tensor_tensor(gn_in[:, sl, 1], gn_sq[:, sl], mv[:, sl, 1], ALU.add).then_inc(gn_stats, 1)

            def gn_finish(k):
                sl = slots(k)
                dve.wait_ge(gn_summed, k + 1)
                nc.vector.tensor_copy(gn_out[:, sl].rearrange("p b s -> p (b s)"),
                                      gn_ps[:, 0:2 * BATCHES[k][1]]).then_inc(gn_read, 1)
                dve.wait_ge(gn_read, k + 1)
                link(nc.vector.tensor_tensor(gn_sq[:, sl], gn_out[:, sl, 0], gn_out[:, sl, 0], ALU.mult))
                nc.vector.tensor_tensor(gn_var[:, sl], gn_out[:, sl, 1], gn_sq[:, sl], ALU.subtract).then_inc(gn_var_ready, 1)
                dve.wait_ge(gn_std_ready, k + 1)
                link(nc.vector.reciprocal(gn_rstd[:, sl], gn_std[:, sl]))
                nc.vector.scalar_tensor_tensor(gn_bias[:, sl], gn_out[:, sl, 0], -1.0, gn_rstd[:, sl],
                                               ALU.mult, ALU.mult).then_inc(gn_ready, 1)

            def value_stats(a):
                dve.wait_ge(values_read, 8 * a + 8)
                for j in range(J):
                    ins = nc.vector.bn_stats(v_stats[:, j, a], v_nat[:, j, :, a, :])
                return ins

            def some_query_stats(a, ks):
                dve.wait_ge(proj_read, 8 * a + 8)
                for k in ks:
                    ins = nc.vector.bn_stats(q_stats[:, k, a], q_nat[:, a % QS, :, k].rearrange("p j g h -> p j (g h)"))
                return ins

            def query_stats(a, done=0):
                some_query_stats(a, range(done, KD)).then_inc(q_stats_done, 1)

            between = {4: lambda: value_stats(0), 5: lambda: query_stats(0), 6: lambda: value_stats(1),
                       8: lambda: (value_stats(2), query_stats(1), query_stats(2))}
            for k in range(len(BATCHES)):
                gn_moments(k)
                gn_finish(k)
                if k in between:
                    between[k]()
            link(value_stats(A - 1))

            for j in range(J):
                ins = nc.vector.bn_aggr(v_mv[:, j], v_stats[:, j].rearrange("p a s -> p (a s)"))
            ins.then_inc(v_var_ready, 1)
            dve.wait_ge(v_std_ready, 1)
            dve.wait_ge(params_loaded, 16 * (2 + 2 * TN))
            link(nc.vector.reciprocal(v_tmp[:], v_std[:]))
            link(nc.vector.tensor_tensor(v_scale[:], v_tmp[:], gam_v[:], ALU.mult))
            link(nc.vector.tensor_tensor(v_tmp[:], v_mv[:, :, 0], v_scale[:], ALU.mult))
            nc.vector.tensor_tensor(v_shift[:], bet_v[:], v_tmp[:], ALU.subtract).then_inc(v_affine, 1)
            some_query_stats(A - 1, range(0, 4))

            def split_lo(slot, off, k, t):
                dve.wait_ge(e_hi_ready, t + 1)
                nc.vector.tensor_tensor(e_lo[:, slot],
                                        e_nat[:, k, off * TN:(off + 1) * TN, :].rearrange("p n (j k) -> p j n k", j=J),
                                        e_hi[:, slot].bitcast(f32), ALU.subtract).then_inc(e_lo_ready, 1)

            split_lo(0, 0, 0, 0)
            for j in range(J):
                dve.wait_ge(v_hi_ready, j + 1)
                nc.vector.tensor_tensor(v_lo[:, j], v_nat[:, j].rearrange("p g a v -> p (g a v)"),
                                        v_hi[:, j].bitcast(f32), ALU.subtract).then_inc(v_lo_ready, 1)
            split_lo(1, 1, 0, 1)
            nc.vector.tensor_reduce(key_max[:], keys[:].rearrange("p j g a k -> p (g a k) j"), AX.X,
                                    ALU.max).then_inc(key_max_ready, 1)
            query_stats(A - 1, done=4)
            split_lo(0, 0, 1, 2)
            dve.wait_ge(key_top_ready, 1)
            for j in range(J):
                kj = keys[:, j].rearrange("p g a k -> p (g a k)")
                nc.vector.tensor_tensor(kj, kj, key_top[:], ALU.subtract).then_inc(keys_shifted, 1)

            dve.wait_ge(q_stats_done, A)
            for k in range(KD):
                ins = nc.vector.bn_aggr(q_mv[:, k], q_stats[:, k].rearrange("p a s -> p (a s)"))
            link(ins)
            link(nc.vector.tensor_tensor(q_sq[:], q_mv[:, :, 0], q_mv[:, :, 0], ALU.mult))
            link(nc.vector.tensor_tensor(q_sq[:], q_sq[:], q_mv[:, :, 1], ALU.add))
            nc.vector.tensor_copy(q_in[:, 0], q_mv[:, :, 0].unsqueeze(1).to_broadcast([P, TN, KD]))
            nc.vector.tensor_copy(q_in[:, 1], q_sq[:].unsqueeze(1).to_broadcast([P, TN, KD])).then_inc(q_moments, 1)
            split_lo(1, 1, 1, 3)
            dve.wait_ge(q_averaged, 1)
            link(nc.vector.tensor_copy(q_out[:], q_ps))
            link(nc.vector.tensor_tensor(q_tmp[:, 2:3], q_out[:, 0:1], q_out[:, 0:1], ALU.mult))
            nc.vector.tensor_tensor(q_tmp[:, 0:1], q_out[:, 1:2], q_tmp[:, 2:3], ALU.subtract).then_inc(q_var_ready, 1)
            dve.wait_ge(q_std_ready, 1)
            link(nc.vector.reciprocal(q_tmp[:, 2:3], q_tmp[:, 1:2]))
            link(nc.vector.tensor_tensor(q_scale[:], q_tmp[:, 2:3], gam_q[:], ALU.mult))
            link(nc.vector.tensor_tensor(q_tmp[:, 3:4], q_out[:, 0:1], q_scale[:], ALU.mult))
            nc.vector.tensor_tensor(q_shift[:], bet_q[:], q_tmp[:, 3:4], ALU.subtract).then_inc(q_affine, 1)
            for i in range(QS):
                dve.wait_ge(q_stored[i], 16 * len(range(i, A, QS)))
            dve.wait_ge(lam_summed, 1)
            link(nc.vector.reciprocal(inv_sum[:], ps_b[:, 1, 0:B // TN]))
            dve.wait_ge(lam_zeroed, 1)
            for g in range(G):
                s, half = g // 2, g % 2
                rows = slice(half * HALF, (half + 1) * HALF)
                nc.vector.scalar_tensor_tensor(
                    lam_diag[rows, g * P:(g + 1) * P].rearrange("p (a v) -> p a v", v=V),
                    ps_b[rows, 0, s * P:(s + 1) * P].rearrange("p (a v) -> p a v", v=V),
                    inv_sum[rows, s:s + 1], row_mask[rows, half * A:(half + 1) * A].unsqueeze(2).to_broadcast([HALF, A, V]),
                    ALU.mult, ALU.mult).then_inc(lam_masked, 1)
            dve.wait_ge(lam_spread, 1)
            link(nc.vector.tensor_copy(content[:], ps_b[:, 1]))

            def read_pos(t, slot):
                dve.wait_ge(pos_summed, t + 1)
                nc.vector.tensor_tensor(pos[:, slot], ps_a[:, slot], content[:], ALU.add).then_inc(pos_ready, 1)

            def add_out(t, slot, off, each=False):
                dve.wait_ge(queried, t + 1)
                for a in range(A):
                    rows = slice(a * V, (a + 1) * V)
                    r = res[rows, :, bass.ds(off, TN)].rearrange("v (g h) n -> v g h n", h=NH)
                    ins = nc.vector.tensor_tensor(
                        r, ps_b[rows, slot, 0:G * HALF].rearrange("v (g a h n) -> v g a h n", g=G, a=2, h=NH)[:, :, a % 2],
                        r, ALU.add)
                    if each:
                        ins.then_inc(res_added, 1)
                if not each:
                    ins.then_inc(res_added, 1)

            for t in range(2):
                dve.wait_ge(pos_copied, t + 1)
                nc.vector.tensor_tensor(pos[:, t], pos[:, t], content[:], ALU.add).then_inc(pos_ready, 1)
            dve.wait_ge(res_loaded, 16 * A)
            add_out(0, 0, 0)

            with dve.Fori(0, TILES // 4 - 1) as q:
                for i in range(4):
                    t = 4 * q + 2 + i
                    read_pos(t, i % 2)
                    split_lo(i % 2, i % 2, i // 2, t + 2)
                    if i == 3:
                        dve.wait_ge(res_loaded, ((q + 1) // (BT // 4) + 1) * (16 * A))
                    add_out(t - 1, (i + 1) % 2, ((t - 1) % (2 * BT)) * TN)
            read_pos(TILES - 2, 0)
            add_out(TILES - 3, 1, 2 * BN - 3 * TN)
            read_pos(TILES - 1, 1)
            add_out(TILES - 2, 0, 2 * BN - 2 * TN)
            add_out(TILES - 1, 1, 2 * BN - TN, each=True)

        @block.tensor
        def _(pe):
            pe.wait_ge(consts, 4)
            pe.wait_ge(weights_loaded, 16 * 3)
            nc.tensor.transpose(ps_a[:, 0, 0:PC], w_rows[:], ident[0:PC, 0:PC]).then_inc(w_transposed, 1)
            pe.wait_ge(consts, 6)

            def gn_average(k, reads):
                pe.wait_ge(gn_stats, k + 1)
                if reads:
                    pe.wait_ge(proj_read, reads)
                nc.tensor.matmul(gn_ps[:, 0:2 * BATCHES[k][1]], group_avg[:], gn_in[:, slots(k)].rearrange("p b s -> p (b s)"),
                                 start=True, stop=True).then_inc(gn_summed, 1)

            def transpose_image(b, i):
                pe.wait_ge(x_normed, b + 1)
                if b >= 2:
                    pe.wait_ge(xt_ready, b - 1)
                for j in range(J):
                    ins = nc.tensor.transpose(ps_a[:, i % 2, j * C:(j + 1) * C], x_in[:, i, j * D:(j + 1) * D], ident[:])
                ins.then_inc(x_transposed, 1)

            def project(b, i):
                pe.wait_ge(xt_ready, b + 1)
                if b == 0 or i % GB == 2:
                    pe.wait_ge(gn_read, 2 if b == 0 else min(b // GB + 3, len(BATCHES)))
                if b >= 2:
                    pe.wait_ge(proj_read, b - 1)
                for j in range(J):
                    ins = nc.tensor.matmul(ps_b[:, i % 2, j * P:j * P + PC], x_t[:, i % 2, j * C:(j + 1) * C], w_cols[:],
                                           start=True, stop=True)
                ins.then_inc(projected, 1)

            gn_average(0, 0)
            pe.wait_ge(gn_read, 1)
            pe.wait_ge(w_ready, 1)
            for a in range(A):
                for i in range(G):
                    b = 8 * a + i
                    transpose_image(b, i)
                    if b == 0:
                        gn_average(1, 0)
                    if b > 0:
                        project(b - 1, (i - 1) % G)
                    if i == 2:
                        gn_average(2 * a + 2, b - 1)
                    if i == 6 and a < A - 1:
                        gn_average(2 * a + 3, b - 1)
            project(B - 1, G - 1)

            def sum_tile(t, slot, first=False, between={}):
                pe.wait_ge(e_hi_ready, t + 1)
                pe.wait_ge(e_lo_ready, t + 1)
                for j in range(J):
                    if first:
                        pe.wait_ge(v_hi_ready, j + 1)
                    if j in between:
                        between[j]()
                    for n, (e, v) in enumerate(((e_hi, v_hi), (e_lo, v_hi), (e_hi, v_lo))):
                        if first and n == 2:
                            pe.wait_ge(v_lo_ready, j + 1)
                        for half in range(BV // BANK):
                            cols = slice(half * BANK, (half + 1) * BANK)
                            ins = nc.tensor.matmul(ps_a[:, slot, cols], e[:, slot, j].rearrange("p n k -> p (n k)"),
                                                   v[:, j, cols], start=(j == 0 and n == 0), stop=(j == J - 1 and n == 2))
                ins.then_inc(pos_summed, 1)

            def query_tile(t, slot):
                pe.wait_ge(pos_ready, t + 1)
                pe.wait_ge(q_diag_ready, t + 1)
                for g in range(G):
                    for half in range(2):
                        cols = slice(g * P + half * HALF, g * P + (half + 1) * HALF)
                        ins = nc.tensor.matmul(ps_b[half * HALF:(half + 1) * HALF, slot, g * HALF:(g + 1) * HALF],
                                               pos[:, slot, cols], q_diag[:, slot, cols], start=True, stop=True)
                ins.then_inc(queried, 1)

            pe.wait_ge(proj_read, B)
            sum_tile(0, 0, first=True)
            sum_tile(1, 1)
            pe.wait_ge(pos_copied, 1)
            sum_tile(2, 0)
            pe.wait_ge(q_moments, 1)
            for s in range(2):
                ins = nc.tensor.matmul(q_ps[:, s:s + 1], q_in[:, s].rearrange("p n k -> p (n k)"), inv_p[:],
                                       start=True, stop=True)
            ins.then_inc(q_averaged, 1)
            pe.wait_ge(keys_exp, J)
            for s in range(B // TN):
                for j in range(J):
                    for half in range(2):
                        nc.tensor.matmul(ps_b[half * HALF:(half + 1) * HALF, 0, s * P:(s + 1) * P],
                                         keys[:, j, 2 * s + half].rearrange("p a k -> p (a k)"),
                                         v_nat[:, j, 2 * s + half].rearrange("p a v -> p (a v)"),
                                         start=(j == 0), stop=(j == J - 1))
            pe.wait_ge(exp_summed, 1)
            for s in range(B // TN):
                ins = nc.tensor.matmul(ps_b[:, 1, s:s + 1], exp_sum[:, s * P:(s + 1) * P], ones[:], start=True, stop=True)
            ins.then_inc(lam_summed, 1)

            def spread_content():
                pe.wait_ge(same_k_ready, 1)
                pe.wait_ge(q_var_ready, 1)
                pe.wait_ge(lam_masked, G)
                for s in range(B // TN):
                    cols = slice(s * TN * V, (s + 1) * TN * V)
                    ins = nc.tensor.matmul(ps_b[:, 1, cols], same_k[:], lam_diag[:, cols], start=True, stop=True)
                ins.then_inc(lam_spread, 1)

            pe.wait_ge(pos_copied, 2)
            sum_tile(3, 1, between={J // 2: spread_content, J - 2: lambda: query_tile(0, 0)})
            query_tile(1, 1)
            query_tile(2, 0)
            with pe.Fori(1, TILES // 4) as q:
                for i in range(4):
                    sum_tile(4 * q + i, i % 2)
                    query_tile(4 * q + i - 1, (i + 1) % 2)
            query_tile(TILES - 1, 1)


_INS = ["x", "L0_conv_Wq", "L0_conv_Wk", "L0_conv_Wv", "L0_conv_E", "L0_conv_gamma_v", "L0_conv_beta_v",
        "L0_conv_gamma_q", "L0_conv_beta_q"]


def kernel(**inputs):
    import numpy as _np
    import concourse.bacc as _bacc
    from concourse import mybir as _mybir
    from concourse.bass_utils import run_bass_kernel_spmd as _run

    nc = _bacc.Bacc("TRN2", target_bir_lowering=False, num_devices=1)
    arrays, args = {}, []
    for name in _INS:
        a = _np.ascontiguousarray(inputs[name])
        arrays[f"in_{name}"] = a
        args.append(nc.dram_tensor(f"in_{name}", a.shape, _mybir.dt.from_np(a.dtype), kind="ExternalInput").ap())
    shape = arrays["in_x"].shape
    args.append(nc.dram_tensor("out_dram", shape, _mybir.dt.float32, kind="ExternalOutput").ap())
    lambda_conv_kernel(nc, *args)
    r = _run(nc, [arrays], core_ids=[0])
    return r.results[0]["out_dram"]
```
